# Optimizing a Trainium2 kernel written in Bass

```python
import numpy as np
import jax
import jax.numpy as jnp

def _softmax(x, axis=-1):
    return jax.nn.softmax(x, axis=axis)

def _gelu(x):
    return jax.nn.gelu(x, approximate=True)

def _silu(x):
    return jax.nn.silu(x)

def _sigmoid(x):
    return jax.nn.sigmoid(x)

def _layernorm(x, axis=-1, eps=1e-05):
    m = jnp.mean(x, axis=axis, keepdims=True)
    v = jnp.var(x, axis=axis, keepdims=True)
    return (x - m) / jnp.sqrt(v + eps)

def _scatter_add(tgt, idx, src, axis=0):
    return tgt.at[idx].add(src)

def _segment_sum(src, seg, n):
    return jax.ops.segment_sum(src, seg, n)
kernel_name = 'mk_adaln_d1_jaxref_r4_51b11c'

def setup_inputs(seed: int=0):
    np.random.seed(seed)
    _w = jnp.asarray

    def _L0_attn_setup():
        import jax, jax.numpy as jnp
        import numpy as np
        EMBED_DIM = 256
        NUM_HEADS = 16
        HEAD_DIM = EMBED_DIM // NUM_HEADS
        key = jax.random.key(seed)
        k1, k2, k3, k4 = jax.random.split(key, 4)
        B, S, D = (2, 512, EMBED_DIM)
        x = jax.random.normal(k1, (B, S, D), dtype=jnp.float32)
        xpos = jax.random.randint(k2, (B, S), 0, 512, dtype=jnp.int32)
        qkv_w = jax.random.normal(k3, (3 * D, D), dtype=jnp.float32) * D ** (-0.5)
        proj_w = jax.random.normal(k4, (D, D), dtype=jnp.float32) * D ** (-0.5)
        proj_b = jnp.zeros((D,), dtype=jnp.float32)
        return {'x': x, 'xpos': xpos, 'qkv_w': qkv_w, 'proj_w': proj_w, 'proj_b': proj_b}
    _L0_attn_in = _L0_attn_setup()

    def _L0_ffn_setup():
        import jax, jax.numpy as jnp
        import numpy as np
        B, T, D, H, R, N = (16, 256, 256, 64, 64, 8)
        key = jax.random.key(seed)
        ks = jax.random.split(key, 8)
        s = lambda k, shape, fan: jax.random.normal(k, shape, jnp.float32) / np.sqrt(fan)
        return {'x': jax.random.normal(ks[0], (B, T, D), jnp.float32), 'W_base': s(ks[1], (D, D), D), 'b_base': jnp.zeros((D,), jnp.float32), 'W_enc': s(ks[2], (N, D, H), D), 'b_enc': jnp.zeros((N, H), jnp.float32), 'W_dec': s(ks[3], (N, H, D), H), 'b_dec': jnp.zeros((N, D), jnp.float32), 'W_down': s(ks[4], (N, D, R), D), 'b_down': jnp.zeros((N, R), jnp.float32), 'W_up': s(ks[5], (N, R, D), R), 'b_up': jnp.zeros((N, D), jnp.float32), 'connected_idx': jnp.arange(N, dtype=jnp.int32)}
    _L0_ffn_in = _L0_ffn_setup()
    _L0_c = _w((lambda *s: np.random.randn(*s).astype(np.float32) * 0.05)(4, 256))
    _L0_wmod = _w((lambda *s: np.random.randn(*s).astype(np.float32) * 0.05)(256, 6 * 256) * 256 ** (-0.5))
    _d = {'L0_attn_x': _L0_attn_in['x'], 'L0_attn_xpos': _L0_attn_in['xpos'], 'L0_attn_qkv_w': _L0_attn_in['qkv_w'], 'L0_attn_proj_w': _L0_attn_in['proj_w'], 'L0_attn_proj_b': _L0_attn_in['proj_b'], 'L0_ffn_W_base': _L0_ffn_in['W_base'], 'L0_ffn_b_base': _L0_ffn_in['b_base'], 'L0_ffn_W_enc': _L0_ffn_in['W_enc'], 'L0_ffn_b_enc': _L0_ffn_in['b_enc'], 'L0_ffn_W_dec': _L0_ffn_in['W_dec'], 'L0_ffn_b_dec': _L0_ffn_in['b_dec'], 'L0_ffn_W_down': _L0_ffn_in['W_down'], 'L0_ffn_b_down': _L0_ffn_in['b_down'], 'L0_ffn_W_up': _L0_ffn_in['W_up'], 'L0_ffn_b_up': _L0_ffn_in['b_up'], 'L0_ffn_connected_idx': _L0_ffn_in['connected_idx'], 'L0_c': _L0_c, 'L0_wmod': _L0_wmod}
    _x0 = _d['L0_attn_x']
    _d['L0_attn_x'] = jax.random.normal(jax.random.fold_in(jax.random.key(seed), 1), (4, 1024, 256), dtype=_x0.dtype)
    del _x0
    return _d

def reference(L0_attn_x, L0_attn_xpos, L0_attn_qkv_w, L0_attn_proj_w, L0_attn_proj_b, L0_ffn_W_base, L0_ffn_b_base, L0_ffn_W_enc, L0_ffn_b_enc, L0_ffn_W_dec, L0_ffn_b_dec, L0_ffn_W_down, L0_ffn_b_down, L0_ffn_W_up, L0_ffn_b_up, L0_ffn_connected_idx, L0_c, L0_wmod):

    def _L0_attn_ref(x, xpos, qkv_w, proj_w, proj_b):
        import jax, jax.numpy as jnp
        import numpy as np
        EMBED_DIM = 256
        NUM_HEADS = 16
        HEAD_DIM = EMBED_DIM // NUM_HEADS
        B, S, D = x.shape
        H, hd = (NUM_HEADS, D // NUM_HEADS)
        scale = hd ** (-0.5)
        qkv = x @ qkv_w.T
        qkv = qkv.reshape(B, S, 3, H, hd)
        qkv = jnp.transpose(qkv, (0, 3, 2, 1, 4))
        q, k, v = (qkv[:, :, 0], qkv[:, :, 1], qkv[:, :, 2])
        scores = jnp.einsum('bhqd,bhkd->bhqk', q, k) * scale
        probs = jax.nn.softmax(scores, axis=-1)
        out = jnp.einsum('bhqk,bhkd->bhqd', probs, v)
        out = jnp.transpose(out, (0, 2, 1, 3)).reshape(B, S, D)
        out = out @ proj_w.T + proj_b
        return out

    def _L0_ffn_ref(x, W_base, b_base, W_enc, b_enc, W_dec, b_dec, W_down, b_down, W_up, b_up, connected_idx):
        import jax, jax.numpy as jnp
        import numpy as np
        B, T, D, H, R, N = (16, 256, 256, 64, 64, 8)
        base = jnp.einsum('btd,de->bte', x, W_base) + b_base
        h = jax.nn.relu(jnp.einsum('btd,ndh->nbth', x, W_enc) + b_enc[:, None, None, :])
        recon = jnp.einsum('nbth,nhd->nbtd', h, W_dec) + b_dec[:, None, None, :]
        losses = jnp.mean((recon - x[None]) ** 2, axis=(2, 3))
        top1 = jnp.argmin(losses, axis=0)
        adp = connected_idx[top1]
        Wd, bd = (W_down[adp], b_down[adp])
        Wu, bu = (W_up[adp], b_up[adp])
        mid = jax.nn.relu(jnp.einsum('btd,bdr->btr', x, Wd) + bd[:, None, :])
        adapter_out = jnp.einsum('btr,brd->btd', mid, Wu) + bu[:, None, :]
        return base + adapter_out
    x = L0_attn_x
    mod = (_silu(L0_c) @ L0_wmod).reshape(L0_c.shape[0], 6, 1, -1)
    sa, ca, ga, sb, cb, gb = (mod[:, 0], mod[:, 1], mod[:, 2], mod[:, 3], mod[:, 4], mod[:, 5])
    ga = (2 * (ga >= 0) - 1) * jnp.maximum(jnp.abs(ga), 0.25)
    gb = (2 * (gb >= 0) - 1) * jnp.maximum(jnp.abs(gb), 0.25)
    h = _layernorm(x, axis=-1) * (1 + ca) + sa
    x = x + ga * _L0_attn_ref(h, L0_attn_xpos, L0_attn_qkv_w, L0_attn_proj_w, L0_attn_proj_b)
    h = _layernorm(x, axis=-1) * (1 + cb) + sb
    x = x + gb * _L0_ffn_ref(h, L0_ffn_W_base, L0_ffn_b_base, L0_ffn_W_enc, L0_ffn_b_enc, L0_ffn_W_dec, L0_ffn_b_dec, L0_ffn_W_down, L0_ffn_b_down, L0_ffn_W_up, L0_ffn_b_up, L0_ffn_connected_idx)
    return x

_drawn_inputs = setup_inputs


def setup_inputs(seed=0):
    import zlib

    import numpy as np

    out = dict(_drawn_inputs(seed))
    spreads = {'L0_attn_proj_b': (0.0, 0.565),
     'L0_ffn_b_base': (0.0, 0.316),
     'L0_ffn_b_enc': (0.0, 0.1),
     'L0_ffn_b_dec': (0.0, 0.1),
     'L0_ffn_b_down': (0.0, 0.472),
     'L0_ffn_b_up': (0.0, 0.343)}
    factors = {'L0_attn_qkv_w': 2.818, 'L0_attn_proj_w': 2.766}
    for name, (base, spread) in spreads.items():
        noise = np.random.default_rng([zlib.crc32(name.encode()), seed]).standard_normal(out[name].shape)
        drawn = base * np.exp(spread * noise) if base else spread * noise
        out[name] = jnp.asarray(drawn.astype(out[name].dtype))
    for name, factor in factors.items():
        out[name] = (out[name] * factor).astype(out[name].dtype)
    return out
```

```python
from contextlib import ExitStack

import concourse.bass as bass
from concourse import mybir

F = mybir.dt.float32
R = mybir.dt.float32r
I32 = mybir.dt.int32
U32 = mybir.dt.uint32
ACT = mybir.ActivationFunctionType
ALU = mybir.AluOpType
AX = mybir.AxisListType

NB, T, D = 4, 1024, 256
NH, HD = 16, 16
NE, H = 8, 64
QC = 48
QM = QC + 2
LA = 3
UB = 64
EPS = 1e-5


class Queue:

    def __init__(self, sem):
        self.sem, self.n, self.ops = sem, 0, []

    def do(self, fn, *after, inc=True):
        self.n += inc
        self.ops.append((after, fn, self.sem if inc else None))
        return (self.sem, self.n)

    def emit(self, eng):
        seen = {}
        for after, fn, sem in self.ops:
            for s, n in after:
                if seen.get(id(s), 0) < n:
                    eng.wait_ge(s, n)
                    seen[id(s)] = n
            ins = fn(eng)
            if sem is not None:
                ins.then_inc(sem, 1)


class Landing:

    def __init__(self, sem):
        self.sem, self.n = sem, 0

    def ev(self):
        return (self.sem, self.n)


def adaln_block(nc, x, wqkvT, wpT, pb, wbase, bbase, wenc, benc, bencc, wdec, wdecT, bdecT,
                wdown, bdown, wup, bup, cidx, cT, wmod, consts, out):
    ctx = ExitStack()
    with ctx:
        def sb(name, shape, dt=F):
            return ctx.enter_context(nc.sbuf_tensor(name, shape, dt))

        def sem(name):
            return ctx.enter_context(nc.semaphore(name))

        pM = ctx.enter_context(nc.psum_tensor("pM", [128, 2, 1024], F))
        pE = ctx.enter_context(nc.psum_tensor("pE", [128, 2, 512], F))
        pO = ctx.enter_context(nc.psum_tensor("pO", [128, 512], F))
        pX = ctx.enter_context(nc.psum_tensor("pX", [128, 512], F))
        modd = nc.dram_tensor("modd", [NB, 6 * D], F, kind="Internal").ap()

        QO = sb("QO", [128, 2, 4, T], R)
        KO = sb("KO", [128, 2, 4, T], R)
        V = sb("V", [128, 2, 8, NH, HD + 1])
        P = sb("P", [128, 2, 4, 512])
        hi = sb("hi", [128, T], R)
        lo = sb("lo", [128, T], R)
        osb = sb("osb", [128, 512])
        Atok = sb("Atok", [128, 8, D])
        xin = sb("xin", [128, 2, D])
        h1T = sb("h1T", [128, 2, T])
        h2T = sb("h2T", [128, 2, T])
        x2 = sb("x2", [128, 8, D])
        X = sb("X", [128, 8, D + 2])
        Hb = sb("Hb", [128, 8, 512])
        mid = sb("mid", [128, 512])
        wqkv_s = sb("wqkv_s", [128, 2, 3 * D])
        wp_s = sb("wp_s", [128, 2, D])
        wpg = sb("wpg", [128, 2, D])
        wb_s = sb("wb_s", [128, 2, D])
        wbg = sb("wbg", [128, 2, D])
        wenc_s = sb("wenc_s", [128, 2, 512])
        wd = sb("wd", [128, 4, D + 2])
        ww = sb("ww", [128, 4, 128])
        wdn = sb("wdn", [128, 2, H])
        bdn = sb("bdn", [H, 1])
        wug = sb("wug", [H + 1, D])
        bbr = sb("bbr", [H + 1, D])
        bc = sb("bc", [128, 4, D])
        pbb = sb("pbb", [128, D])
        nbe = sb("nbe", [128, 512])
        cst = sb("cst", [128, 138])
        cT_s = sb("cT_s", [128, 2, NB])
        sg = sb("sg", [128, 3, 2 * NB])
        modT = sb("modT", [128, 4, NB])
        ones = sb("ones", [128, 8])
        st1 = sb("st1", [128, 2, 6])
        mv1 = sb("mv1", [128, 2, 2])
        rs1 = sb("rs1", [128, 2, 2])
        st2 = sb("st2", [128, 8, 6])
        mv2 = sb("mv2", [128, 8, 2])
        rs2 = sb("rs2", [128, 2, 8])
        nh = sb("nh", [128, 8])
        mx = sb("mx", [128, 2, 16])
        mhl = sb("mhl", [128, 2, 32])
        mh = sb("mh", [128, 16], R)
        mT = sb("mT", [32, 2, 128])
        rec = sb("rec", [128, 4, 4])
        junk = sb("junk", [128, 258])
        junk2 = sb("junk2", [128, 256])
        accC = sb("accC", [128, 4])
        accA = sb("accA", [128, 4])
        ps = sb("ps", [128, 4])
        pl8 = sb("pl8", [128, 4, 2])
        xsq = sb("xsq", [128, 8])
        xsq1 = sb("xsq1", [128, 1])
        xbar = sb("xbar", [128, 2, 2])
        bT = sb("bT", [128, 2, 8])
        bTm = sb("bTm", [128, 2, 8])
        bTq = sb("bTq", [128, 2, 8])
        be = sb("be", [128, 4, 8])
        bec = sb("bec", [128, 4])
        bdT = sb("bdT", [128, 2, 8])
        trow = sb("trow", [1, 8])
        connf = sb("connf", [1, 8])
        conni = sb("conni", [1, 8], I32)
        sel = sb("sel", [1, 8, 8])
        selu = sb("selu", [1, 8], U32)
        seli = sb("seli", [1, 1], I32)

        ident = cst[:, 0:128]
        bmask = cst[:, 128:130]
        iota8 = cst[0:1, 130:138]
        wmod_s = Hb[:, 0:6, :].rearrange("p a b -> p (a b)").rearrange("p (c n) -> p c n", c=2)
        wdT_s = Hb[:, 6:8, :]
        AT = Hb[:, 0:4, :].rearrange("p a b -> p (a b)").rearrange("p (c n) -> p c n", c=2)
        gt = Atok[0:NB, 0:4, :].rearrange("p (a b) n -> p a b n", a=2)
        modr = X[0:NB, :, :].rearrange("p a b -> p (a b)")
        pMf = pM[:, :, :].rearrange("p a b -> p (a b)")

        pe, act, dve, pool = (Queue(sem(n)) for n in ("s_pe", "s_act", "s_dve", "s_pool"))
        sp = Queue(None)
        places = {}

        def dma(place, dst, src, *after):
            if place not in places:
                places[place] = Landing(sem("d_" + place))
            p = places[place]
            p.n += 16
            sp.do(lambda e: e.dma_start(dst, src).then_inc(p.sem, 16), *after, inc=False)
            return p.ev()

        def mm(outp, lhsT, rhs, *after, start=True, stop=True, inc=True, skip=False):
            return pe.do(lambda e: e.matmul(outp, lhsT, rhs, start=start, stop=stop,
                                            skip_group_check=skip), *after, inc=inc)

        def tr(outp, in_, idn, *after, inc=True):
            return pe.do(lambda e: e.transpose(outp, in_, idn), *after, inc=inc)

        ev_cst = dma("cst", cst[:, :], consts)
        ev_cT = dma("cT", cT_s[:, :, :], cT.rearrange("(c p) b -> p c b", p=128))
        x_tiles = x.rearrange("b (t p) d -> b p t d", p=128)
        ev_xin = dma("xin", xin[:, :, :], x_tiles[0, :, 0:2, :])
        ev_wmod = dma("wmod", wmod_s, wmod.rearrange("(c p) n -> p c n", p=128))
        ev_wqkv = dma("wqkv", wqkv_s[:, :, :], wqkvT.rearrange("(c p) n -> p c n", p=128))

        def load_ffn_weights():
            evs = [
                dma("w0", wd[:, :, 0:D], wdec.rearrange("(c p) n -> p c n", p=128)),
                dma("w1", wdT_s, wdecT.rearrange("(c p) n -> p c n", p=128)),
                dma("w2", bec[:, :], bencc),
                dma("w3", bdT[:, :, :], bdecT.rearrange("(c p) n -> p c n", p=128)),
                dma("w4", wp_s[:, :, :], wpT.rearrange("(c p) n -> p c n", p=128)),
                dma("w5", wb_s[:, :, :], wbase.rearrange("(c p) n -> p c n", p=128)),
                dma("w6", wenc_s[:, :, :], wenc.rearrange("(c p) n -> p c n", p=128)),
                dma("w7", pbb[:, :], pb.to_broadcast([128, D])),
                dma("w8", nbe[:, :], benc.to_broadcast([128, 512])),
                dma("w9", bbr[H:H + 1, :], bbase),
                dma("w10", conni[:, :], cidx),
            ]
            return evs

        ev_ones = pool.do(lambda e: e.memset(ones[:, :], 1.0))
        ev_nh = pool.do(lambda e: e.memset(nh[:, :], -0.5))
        ev_vone = pool.do(lambda e: e.memset(V[:, :, :, :, HD:], 1.0))
        ev_mid1 = dve.do(lambda e: e.memset(mid[H:H + 1, :], 1.0))
        pf = P[0:2, :, :, :].rearrange("p a b n -> p (a b n)")
        ev_pone = pool.do(lambda e: e.memset(pf, 1.0), ev_vone)
        for half in (0, 1):
            for slot in (0, 1):
                ev_kone = dma("kone", KO[64 * half + QC:64 * half + QM, slot, :, :].bitcast(F), pf, ev_pone)

        ev_po = dve.do(lambda e: e.memset(pO[:, :], 0.0))

        c8 = cT_s[:, :, :].rearrange("p a b -> p (a b)")
        e1 = act.do(lambda e: e.activation(sg[:, 0, :], c8, ACT.Exp, scale=-1.0), ev_cT)
        e2 = dve.do(lambda e: e.tensor_scalar(sg[:, 1, :], sg[:, 0, :], 1.0, None, ALU.add), e1)
        e3 = dve.do(lambda e: e.reciprocal(sg[:, 2, :], sg[:, 1, :]), e2)
        e4 = dve.do(lambda e: e.tensor_tensor(sg[:, 0, :], sg[:, 2, :], c8, ALU.mult), e3)
        mod_ev = []
        for j in range(3):
            for c in range(2):
                ev = mm(pMf[0:NB, 512 * j:512 * j + 512], sg[:, 0, NB * c:NB * c + NB],
                        wmod_s[:, c, 512 * j:512 * j + 512], e4, ev_wmod, start=c == 0, stop=c == 1,
                        inc=c == 1)
            mod_ev.append(act.do(lambda e, j=j: e.activation(modr[:, 512 * j:512 * j + 512],
                                                             pMf[0:NB, 512 * j:512 * j + 512], ACT.Copy), ev))
        mod_free = mod_ev[-1]
        evc = dve.do(lambda e: e.tensor_scalar(modr[:, 256:512], modr[:, 256:512], 1.0, None, ALU.add), mod_ev[0])
        evb = dve.do(lambda e: e.tensor_scalar(modr[:, 1024:1280], modr[:, 1024:1280], 1.0, None, ALU.add),
                     mod_ev[2])
        evg = []
        for k, o in ((0, 512), (1, 1280)):
            a = dve.do(lambda e, k=k, o=o: e.tensor_scalar(gt[:, k, 0, :], modr[:, o:o + 256], 0.0, 2.0,
                                                           ALU.is_ge, ALU.mult), mod_ev[2])
            a = dve.do(lambda e, k=k, o=o: e.scalar_tensor_tensor(
                out=gt[:, k, 1, :], in0=modr[:, o:o + 256], scalar=-1.0, in1=modr[:, o:o + 256],
                op0=ALU.mult, op1=ALU.max))
            a = dve.do(lambda e, k=k: e.tensor_scalar(gt[:, k, 1, :], gt[:, k, 1, :], 0.25, None, ALU.max), a)
            evg.append(dve.do(lambda e, k=k, o=o: e.scalar_tensor_tensor(
                out=modr[:, o:o + 256], in0=gt[:, k, 0, :], scalar=-1.0, in1=gt[:, k, 1, :],
                op0=ALU.add, op1=ALU.mult), a))
        ev_modd = dma("modd", modd, modr[:, 0:6 * D], evc, evb, *evg)
        for k in range(4):
            evt = tr(pX[:, NB * k:NB * k + NB], modr[:, 128 * k:128 * k + 128], ident[0:NB, 0:NB],
                     evc, ev_cst, inc=k == 3)
        ev_modT = dve.do(lambda e: e.tensor_copy(modT[:, :, :].rearrange("p a b -> p (a b)"), pX[:, 0:16]), evt)

        last = {"pX": ev_modT, "P": [ev_kone] * 2, "E": [None] * 2, "M": [mod_free] * 2, "pO": ev_po,
                "hilo_in": None, "xin": ev_xin}

        def after(*evs):
            return [e for e in evs if e is not None]

        h1_ready = [[None] * 4 for _ in range(NB)]
        h1_read = [None]
        xin_free = [None]

        def ln1_load(b, k):
            def f():
                if (b, k) != (0, 0):
                    last["xin"] = dma("xin", xin[:, :, :], x_tiles[b, :, 2 * k:2 * k + 2, :],
                                      *after(xin_free[0]))
            return f

        def ln1_stats(b, k):
            def f():
                for t in range(2):
                    a = dve.do(lambda e, t=t: e.bn_stats(st1[:, t, :], xin[:, t, :]), last["xin"])
                for t in range(2):
                    a = dve.do(lambda e, t=t: e.bn_aggr(mv1[:, t, :], st1[:, t, :]), a)
                a = pool.do(lambda e: e.tensor_scalar(rs1[:, 0, :], mv1[:, :, 1], EPS, None, ALU.add), a, ev_pone)
                a = pool.do(lambda e: e.tensor_tensor(rs1[:, 1, :], rs1[:, 0, :], nh[:, 0:2], ALU.pow), a)
                last["rs1"] = a
            return f

        def ln1_norm(b, k):
            def f():
                for t in range(2):
                    a = dve.do(lambda e, t=t: e.tensor_scalar(xin[:, t, :], xin[:, t, :], mv1[:, t, 0:1],
                                                              rs1[:, 1, t:t + 1], ALU.subtract, ALU.mult),
                               last["rs1"])
                last["xn"] = a
            return f

        def ln1_turn(b, k):
            def f():
                for c in range(2):
                    for t in range(2):
                        a = tr(pX[:, 256 * c + 128 * t:256 * c + 128 * t + 128],
                               xin[:, t, 128 * c:128 * c + 128], ident, last["xn"], last["pX"],
                               inc=c == 1 and t == 1)
                xin_free[0] = a
                for c in range(2):
                    g = act.do(lambda e, c=c: e.activation(
                        h1T[:, c, 256 * k:256 * k + 256], pX[:, 256 * c:256 * c + 256], ACT.Identity,
                        bias=modT[:, c, b:b + 1], scale=modT[:, 2 + c, b:b + 1]),
                        *after(a, ev_modT, h1_read[0]))
                last["pX"] = g
                h1_ready[b][k] = g
            return f

        oct_ready = {}
        e_done = {}

        def qk_group(b, o, w, half):
            def f():
                r0 = 256 * w + 128 * o
                for c in range(2):
                    a = mm(pX[:, :], wqkv_s[:, c, r0:r0 + 128], h1T[:, c, 512 * half:512 * half + 512],
                           ev_wqkv, last["pX"], h1_ready[b][2 * half + 1], start=c == 0, stop=c == 1,
                           inc=c == 1)
                h1_read[0] = a
                cs = slice(512 * half, 512 * half + 512)
                sc = 0.25 if w == 0 else 1.0
                a = act.do(lambda e: e.activation(hi[:, cs], pX[:, :], ACT.Copy, scale=sc),
                           *after(a, last["hilo_in"]))
                a = dve.do(lambda e: e.scalar_tensor_tensor(out=lo[:, cs], in0=pX[:, :], scalar=sc,
                                                            in1=hi[:, cs].bitcast(F), op0=ALU.mult,
                                                            op1=ALU.subtract), a)
                last["pX"] = a
                if half == 1:
                    slot = (2 * b + o) % 2
                    dst = KO if w else QO
                    parts = (hi, lo, hi) if w else (hi, hi, lo)
                    n = 2 * b + o
                    for h in range(8):
                        for r in range(3):
                            p0 = 64 * (h % 2) + 16 * r
                            ev = dma(f"op{w}{slot}", dst[p0:p0 + 16, slot, h // 2, :].bitcast(F),
                                     parts[r][16 * h:16 * h + 16, :].bitcast(F),
                                     *after(a, ev_kone, e_done.get(n - 2)))
                    last["hilo_in"] = ev
                    oct_ready[(n, w)] = ev
            return f

        v_ready = {}
        pv_done = {}

        def v_group(b, k):
            def f():
                for t in range(2):
                    for c in range(2):
                        tt = 2 * k + t
                        a = mm(pX[:, 256 * t:256 * t + 256], h1T[:, c, 128 * tt:128 * tt + 128],
                               wqkv_s[:, c, 512:768], ev_wqkv, last["pX"], h1_ready[b][k],
                               start=c == 0, stop=c == 1, inc=c == 1 and t == 1)
                h1_read[0] = a
                a = act.do(lambda e: e.activation(V[:, b % 2, 2 * k:2 * k + 2, :, 0:HD],
                                                  pX[:, :].rearrange("p (t h e) -> p t h e", t=2, e=HD), ACT.Copy),
                           *after(a, pv_done.get(b - 2)))
                last["pX"] = a
                v_ready[(b, k)] = a
            return f

        m_count = [0]
        m_last = {}
        m_rows = {}
        mx_free = [None, None]

        def operand(buf, gi, j, rows, sl):
            base = 64 * (j % 2)
            return buf[base:base + rows, (gi // 2) % 2, 2 * (gi % 2) + j // 2, sl]

        def m_tile(i):
            hq, k = divmod(i, 16)
            gi, c = divmod(hq, 2)
            j, qb = divmod(k, 4)
            s = m_count[0] % 2
            m_count[0] += 1
            q0 = 512 * c + 128 * qb
            n = gi // 2
            for kh in range(2):
                a = mm(pM[:, s, 512 * kh:512 * kh + 512], operand(QO, gi, j, QC, slice(q0, q0 + 128)),
                       operand(KO, gi, j, QC, slice(512 * kh, 512 * kh + 512)), last["M"][s],
                       oct_ready[(n, 0)], oct_ready[(n, 1)], inc=kh == 1)
            g = dve.do(lambda e: e.tensor_reduce(mx[:, hq % 2, k:k + 1], pM[:, s, :], AX.X, ALU.max,
                                                 negate=True), *after(a, mx_free[hq % 2]))
            last["M"][s] = g
            if k == 15:
                a = dve.do(lambda e: e.tensor_copy(mh[:, :], mx[:, hq % 2, :]), g)
                dve.do(lambda e: e.tensor_copy(mhl[:, hq % 2, 0:16], mh[:, :].bitcast(F)), a)
                m_last[hq] = dve.do(lambda e: e.tensor_tensor(mhl[:, hq % 2, 16:32], mx[:, hq % 2, :],
                                                              mh[:, :].bitcast(F), ALU.subtract), a)
                mx_free[hq % 2] = m_last[hq]

        def m_turn(hq):
            gi, c = divmod(hq, 2)
            a = tr(pX[0:32, 0:128], mhl[:, hq % 2, :], ident, m_last[hq], last["pX"])
            mx_free[hq % 2] = a
            a = act.do(lambda e: e.activation(mT[:, hq % 2, :], pX[0:32, 0:128], ACT.Copy),
                       *after(a, m_rows.get(hq - 2)))
            last["pX"] = a
            for r in range(2):
                for j in range(4):
                    p0 = 64 * (j % 2) + QC + r
                    dst = QO[p0:p0 + 1, (gi // 2) % 2, 2 * (gi % 2) + j // 2, 512 * c:512 * c + 512]
                    ev = dma(f"m{hq % 2}", dst.rearrange("p (a b) -> p a b", a=4).bitcast(F),
                             mT[16 * r + 4 * j:16 * r + 4 * j + 4, hq % 2, :], a)
            m_rows[hq] = ev

        e_count = [0]
        exp_ev = {}

        def e_tile(U, j):
            gi, u = divmod(U, 16)
            c, kb = divmod(u, 8)
            s = e_count[0] % 2
            e_count[0] += 1
            a = mm(pE[:, s, :], operand(KO, gi, j, QM, slice(128 * kb, 128 * kb + 128)),
                   operand(QO, gi, j, QM, slice(512 * c, 512 * c + 512)),
                   *after(m_rows[2 * gi + c], last["E"][s], oct_ready[(gi // 2, 0)], oct_ready[(gi // 2, 1)]))
            e_done[gi // 2] = a
            g = act.do(lambda e: e.activation(P[:, U % 2, j, :], pE[:, s, :], ACT.Exp),
                       *after(a, last["P"][U % 2]))
            last["E"][s] = g
            exp_ev[U] = g

        def pv(U):
            gi, u = divmod(U, 16)
            kb = u % 8
            b = gi // 4
            for j in range(4):
                h = 4 * (gi % 4) + j
                a = mm(pO[32 * j:32 * j + HD + 1, :], V[:, b % 2, kb, h, :], P[:, U % 2, j, :],
                       *after(exp_ev[U], v_ready[(b, kb // 2)], ev_vone, last["pO"] if kb == 0 else None),
                       start=kb == 0, stop=kb == 7, inc=j == 3)
            last["P"][U % 2] = a
            pv_done[b] = a
            if kb == 7:
                a = act.do(lambda e: e.activation(osb[:, :], pO[:, :], ACT.Copy), *after(a, last.get("osb")))
                last["pO"] = a
                last["osb_in"] = a

        at_ev = {}

        def o_turn(U):
            gi, u = divmod(U, 16)
            c, b, g = u // 8, gi // 4, gi % 4
            for k in range(4):
                a = tr(pX[:, 128 * k:128 * k + 128], osb[:, 128 * k:128 * k + 128], ident,
                       last["osb_in"], last["pX"], inc=k == 3)
            last["osb"] = a
            v = pX[:, :].rearrange("p (k j e) -> p k j e", k=4, j=4)
            a = dve.do(lambda e: e.reciprocal(rec[:, :, :], v[:, :, :, HD]), a)
            dst = Atok[:, 4 * c:4 * c + 4, 64 * g:64 * g + 64].rearrange("p k (j e) -> p k j e", j=4)
            a = dve.do(lambda e: e.tensor_tensor(
                dst, v[:, :, :, 0:HD], rec[:, :, :].unsqueeze(3).to_broadcast([128, 4, 4, HD]), ALU.mult),
                *after(a, at_ev.get((b - 1, 3))))
            last["pX"] = a
            last["Atok"] = a

        st = {}

        def at_turn(b, k):
            def f():
                c, th = k // 2, k % 2
                for t in range(4):
                    a = tr(pX[:, 128 * t:128 * t + 128], Atok[:, 4 * th + t, 128 * c:128 * c + 128], ident,
                           last["Atok"], last["pX"], inc=t == 3)
                at_ev[(b, k)] = a
                a = act.do(lambda e: e.activation(AT[:, c, 512 * th:512 * th + 512], pX[:, :], ACT.Copy),
                           *after(a, st.get("Hread"), st.get("setup")))
                last["pX"] = a
                st["AT"] = a
            return f

        def prep(b):
            def f():
                for k, o in enumerate((512, 768, 1024, 1280)):
                    st["bc"] = dma("bc", bc[:, k, :], modd[b:b + 1, o:o + 256].to_broadcast([128, 256]),
                                   *after(ev_modd, st.get("bc_read")))
                ev = dma("x2", x2[:, :, :], x_tiles[b], *after(st.get("x2_out")))
                ga = bc[:, 0:1, :].to_broadcast([128, 2, D])
                gb = bc[:, 3:4, :].to_broadcast([128, 2, D])
                a = pool.do(lambda e: e.tensor_tensor(wpg[:, :, :], wp_s[:, :, :], ga, ALU.mult),
                            *after(st["bc"], st["w"][4], st.get("proj")))
                a = pool.do(lambda e: e.tensor_tensor(bc[:, 0, :], pbb[:, :], bc[:, 0, :], ALU.mult), a,
                            st["w"][7])
                pool.do(lambda e: e.tensor_tensor(wbg[:, :, :], wb_s[:, :, :], gb, ALU.mult), st["w"][5],
                        *after(st.get("outmm")))
                for t in range(8):
                    st["x2"] = pool.do(lambda e, t=t: e.tensor_tensor(x2[:, t, :], x2[:, t, :], bc[:, 0, :],
                                                                      ALU.add), ev, a)
            return f

        def proj(b, k):
            def f():
                for t in range(2):
                    for c in range(2):
                        tt = 2 * k + t
                        a = mm(pX[:, 256 * t:256 * t + 256], AT[:, c, 128 * tt:128 * tt + 128], wpg[:, c, :],
                               st["AT"], st["x2"], last["pX"], start=c == 0, stop=c == 1,
                               inc=c == 1 and t == 1)
                st["proj"] = a
                sl = x2[:, 2 * k:2 * k + 2, :]
                a = dve.do(lambda e: e.tensor_tensor(sl, pX[:, :].rearrange("p (t n) -> p t n", t=2), sl,
                                                     ALU.add), a)
                last["pX"] = a
                for t in range(2):
                    st["st2"] = dve.do(lambda e, t=t: e.bn_stats(st2[:, 2 * k + t, :], x2[:, 2 * k + t, :]), a)
            return f

        def ln2_stats(b):
            def f():
                a = st["st2"]
                for t in range(8):
                    a2 = dve.do(lambda e, t=t: e.bn_aggr(mv2[:, t, :], st2[:, t, :]), a)
                a = pool.do(lambda e: e.tensor_scalar(rs2[:, 0, :], mv2[:, :, 1], EPS, None, ALU.add), a2)
                st["rs2"] = pool.do(lambda e: e.tensor_tensor(rs2[:, 1, :], rs2[:, 0, :], nh[:, :], ALU.pow), a)
                if b == 0:
                    st["xone"] = pool.do(lambda e: e.memset(X[:, :, D:D + 2], 1.0), ev_modd, evt)
            return f

        def ln2_norm(b, k):
            def f():
                evs = []
                for t in (2 * k, 2 * k + 1):
                    evs.append(dve.do(lambda e, t=t: e.scalar_tensor_tensor(
                        out=X[:, t, 0:D], in0=x2[:, t, :], scalar=mv2[:, t, 0:1], in1=bc[:, 2, :],
                        op0=ALU.subtract, op1=ALU.mult), *after(st["rs2"], st["bc"], st.get("Xread"), ev_modd, evt)))
                for i, t in enumerate((2 * k, 2 * k + 1)):
                    a = dve.do(lambda e, t=t: e.scalar_tensor_tensor(
                        out=X[:, t, 0:D], in0=X[:, t, 0:D], scalar=rs2[:, 1, t:t + 1], in1=bc[:, 1, :],
                        op0=ALU.mult, op1=ALU.add), evs[i])
                st["X"] = a
                for t in (2 * k, 2 * k + 1):
                    g = act.do(lambda e, t=t: e.activation(junk2[:, :], X[:, t, 0:D], ACT.Square,
                                                           accum_out=xsq[:, t:t + 1]),
                               *after(a, st.get("xsq"), st.get("xsq_read")))
                    st["xsq"] = g
            return f

        def x_turn(b, k):
            def f():
                c, th = k % 2, k // 2
                for t in range(4):
                    a = tr(pX[:, 128 * t:128 * t + 128], X[:, 4 * th + t, 128 * c:128 * c + 128], ident,
                           st["X"], last["pX"], inc=t == 3)
                a = act.do(lambda e: e.activation(h2T[:, c, 512 * th:512 * th + 512], pX[:, :], ACT.Identity,
                                                  accum_out=xbar[:, c, th:th + 1]),
                           *after(a, st.get("outmm"), st.get("Lmm")))
                last["pX"] = a
                st[("h2T", th)] = a
            return f

        def enc(b, t):
            def f():
                for c in range(2):
                    a = mm(pX[:, :], h2T[:, c, 128 * t:128 * t + 128], wenc_s[:, c, :], st[("h2T", t // 4)],
                           st["w"][6], last["pX"], start=c == 0, stop=c == 1, inc=c == 1)
                a = dve.do(lambda e: e.tensor_tensor(Hb[:, t, :], pX[:, :], nbe[:, :], ALU.max),
                           *after(a, st["nbe"], st["proj"], st.get("Hread")))
                last["pX"] = a
                st["H"] = a
            return f

        def gram_c(b, p):
            def f():
                for t in range(8):
                    a = mm(pX[:, 0:D + 2], Hb[:, t, 128 * p:128 * p + 128], X[:, t, :], st["H"], last["pX"],
                           st["xone"], start=t == 0, stop=t == 7, inc=t == 7)
                st["Xread"] = a
                a = dve.do(lambda e: e.tensor_tensor_reduce(junk[:, :], pX[:, 0:D + 2], wd[:, p, :], 1.0, 0.0,
                                                            ALU.mult, ALU.add, accC[:, p:p + 1]),
                           *after(a, st["wd"], st.get("junk"), st.get("acc_read")))
                last["pX"] = a
                st["junk"] = a
            return f

        def gram_a(b, p):
            def f():
                for t in range(8):
                    a = mm(pX[:, 0:128], Hb[:, t, 128 * p:128 * p + 128], Hb[:, t, 128 * p:128 * p + 128],
                           st["H"], last["pX"], start=t == 0, stop=t == 7, inc=t == 7)
                st["Hread"] = a
                a = dve.do(lambda e: e.tensor_tensor_reduce(junk[:, 0:128], pX[:, 0:128], ww[:, p, :], 1.0, 0.0,
                                                            ALU.mult, ALU.add, accA[:, p:p + 1]),
                           *after(a, st["ww"], st.get("junk"), st.get("acc_read")))
                last["pX"] = a
                st["junk"] = a
            return f

        def select(b):
            def f():
                a = dve.do(lambda e: e.tensor_tensor(ps[:, :], accC[:, :], accA[:, :], ALU.add),
                           *after(st["junk"], st.get("Lmm")))
                st["acc_read"] = a
                g = dve.do(lambda e: e.tensor_reduce(xsq1[:, :], xsq[:, :], AX.X, ALU.add),
                           *after(st["xsq"], st.get("Lmm")))
                st["xsq_read"] = g
                a = dve.do(lambda e: e.tensor_tensor(
                    pl8[:, :, :], ps[:, :].unsqueeze(2).to_broadcast([128, 4, 2]),
                    bmask.unsqueeze(1).to_broadcast([128, 4, 2]), ALU.mult), a)
                L = pX[0:1, 0:8]
                mm(L, ones[:, 0:1], pl8[:, :, :].rearrange("p a b -> p (a b)"), a, last["pX"], ev_ones,
                   stop=False, inc=False)
                for c in range(2):
                    for th in range(2):
                        mm(L, xbar[:, c, th:th + 1], bTm[:, c, :], st[("h2T", 0)], st[("h2T", 1)], st["bTm"],
                           start=False, stop=False, inc=False)
                mm(L, xsq1[:, 0:1], ones[:, :], g, start=False, stop=False, inc=False)
                a = mm(L, ones[0:1, 0:1], trow[:, :], st["trow"], start=False)
                st["Lmm"] = a
                a = dve.do(lambda e: e.tensor_scalar(sel[:, 0, :], L, -1.0 / (T * D), None, ALU.mult),
                           *after(a, st.get("seli_read")))
                last["pX"] = a
                a = dve.do(lambda e: e.max(sel[:, 1, :], sel[:, 0, :]), a)
                a = dve.do(lambda e: e.max_index(selu[:, :], sel[:, 1, :], sel[:, 0, :]), a)
                a = dve.do(lambda e: e.tensor_copy(sel[:, 2, 0:1], selu[:, 0:1]), a)
                a = dve.do(lambda e: e.tensor_scalar(sel[:, 3, :], iota8, sel[:, 2, 0:1], None, ALU.is_equal), a)
                a = dve.do(lambda e: e.tensor_tensor_reduce(sel[:, 4, :], sel[:, 3, :], connf[:, :], 1.0, 0.0,
                                                            ALU.mult, ALU.add, sel[:, 5, 0:1]),
                           a, st["conn"])
                a = dve.do(lambda e: e.tensor_scalar(sel[:, 5, 1:2], sel[:, 5, 0:1], 0.0, 8.0, ALU.is_lt,
                                                     ALU.mult), a)
                a = dve.do(lambda e: e.tensor_tensor(sel[:, 5, 2:3], sel[:, 5, 0:1], sel[:, 5, 1:2], ALU.add), a)
                a = dve.do(lambda e: e.tensor_scalar(seli[:, :], sel[:, 5, 2:3], 0.0, 7.0, ALU.max, ALU.min), a)
                st["idx"] = a
            return f

        def fetch(b):
            def f():
                vals = {}

                def dyn(place, dst, src, *evs):
                    if place not in places:
                        places[place] = Landing(sem("d_" + place))
                    p = places[place]
                    p.n += 16
                    sp.do(lambda e: e.dma_start(dst, src(vals["v"])).then_inc(p.sem, 16), *evs, inc=False)
                    return p.ev()

                def load(e):
                    vals["v"] = e.value_load(seli[0:1, 0:1], min_val=0, max_val=7)
                sp.do(load, st["idx"], inc=False)
                w = after(st.get("midmm"), st.get("outmm"), st.get("relu"))
                e1 = dyn("sel", wdn[:, :, :], lambda v: wdown[bass.ds(v, 1), :, :].rearrange(
                    "a (c p) r -> p (a c) r", p=128), *w)
                e1 = dyn("sel", bdn[:, :], lambda v: bdown[bass.ds(v, 1), :].rearrange("a r -> r a"))
                e1 = dyn("sel", wug[0:H, :], lambda v: wup[bass.ds(v, 1), :, :].rearrange("a r n -> (a r) n"))
                e1 = dyn("sel", wug[H:H + 1, :], lambda v: bup[bass.ds(v, 1), :])
                st["sel"] = e1
                a = dve.do(lambda e: e.tensor_tensor(wug[H:H + 1, :], wug[H:H + 1, :], bbr[H:H + 1, :],
                                                     ALU.add), e1, st["w"][9])
                a = dve.do(lambda e: e.tensor_tensor(wug[:, :], wug[:, :], bc[0:H + 1, 3, :], ALU.mult), a)
                st["wug"] = a
                st["seli_read"] = e1
                st["bc_read"] = a
            return f

        def mid_mm(b, half):
            def f():
                for c in range(2):
                    a = mm(pX[0:H, :], wdn[:, c, :], h2T[:, c, 512 * half:512 * half + 512], st["sel"],
                           last["pX"], start=c == 0, stop=c == 1, inc=c == 1)
                st["midmm"] = a
                a = act.do(lambda e: e.activation(mid[0:H, :], pX[0:H, :], ACT.Relu, bias=bdn[:, 0:1]),
                           *after(a, st.get("outmm")))
                last["pX"] = a
                st["mid"] = a
                st["relu"] = a
            return f

        def out_mm(b, k):
            def f():
                for t in range(2):
                    tt = 2 * k + t
                    o = pX[:, 256 * t:256 * t + 256]
                    for c in range(2):
                        mm(o, h2T[:, c, 128 * tt:128 * tt + 128], wbg[:, c, :], last["pX"], st["x2"],
                           start=c == 0, stop=False, inc=False)
                    m0 = 128 * (tt % 4)
                    a = mm(o, mid[0:H + 1, m0:m0 + 128], wug[:, :], st["mid"], st["wug"], ev_mid1,
                           start=False, inc=t == 1)
                st["outmm"] = a
                sl = x2[:, 2 * k:2 * k + 2, :]
                a = dve.do(lambda e: e.tensor_tensor(sl, pX[:, :].rearrange("p (t n) -> p t n", t=2), sl,
                                                     ALU.add), a)
                last["pX"] = a
                st["x2_out"] = dma("out", out.rearrange("b (t p) d -> b p t d", p=128)[b, :, 2 * k:2 * k + 2, :],
                                   sl, a)
            return f

        def setup_a():
            a = dve.do(lambda e: e.memset(be[:, :, :], 0.0))
            for p in range(4):
                g = dve.do(lambda e, p=p: e.tensor_scalar(be[:, p, 2 * p:2 * p + 2], bmask, bec[:, p:p + 1],
                                                          None, ALU.mult), a, st["w"][2], ev_cst)
            for c in range(2):
                for p in range(4):
                    a = mm(pX[:, 8 * c:8 * c + 8], wd[:, p, 128 * c:128 * c + 128], be[:, p, :], g,
                           st["w"][0], last["pX"], start=p == 0, stop=p == 3, inc=p == 3)
            a = dve.do(lambda e: e.tensor_tensor(bT[:, :, :], pX[:, 0:16].rearrange("p (c n) -> p c n", c=2),
                                                 bdT[:, :, :], ALU.add), a, st["w"][3])
            last["pX"] = a
            st["bT"] = a
            st["bTm"] = dve.do(lambda e: e.tensor_scalar(bTm[:, :, :], bT[:, :, :], -2.0, None, ALU.mult), a)
            st["bTq"] = dve.do(lambda e: e.tensor_tensor(bTq[:, :, :], bT[:, :, :], bT[:, :, :], ALU.mult))
            a = dve.do(lambda e: e.tensor_copy(connf[:, :], conni[:, :]), st["w"][10])
            st["conn"] = a
            st["nbe"] = dve.do(lambda e: e.tensor_scalar(nbe[:, :], nbe[:, :], -1.0, None, ALU.mult), st["w"][8])

        def setup_b():
            for p in range(4):
                for c in range(2):
                    a = mm(pX[:, 8 * p:8 * p + 8], wdT_s[:, c, 128 * p:128 * p + 128], bT[:, c, :], st["bT"],
                           st["w"][1], last["pX"], start=c == 0, stop=c == 1, inc=c == 1)
            for p in range(4):
                g = dve.do(lambda e, p=p: e.scalar_tensor_tensor(
                    out=pl8[:, p, :], in0=pX[:, 10 * p:10 * p + 2], scalar=2.0, in1=bmask, op0=ALU.mult,
                    op1=ALU.mult), a)
            last["pX"] = g
            g = dve.do(lambda e: e.tensor_reduce(wd[:, :, D], pl8[:, :, :], AX.X, ALU.add), g)
            g = dve.do(lambda e: e.memset(wd[:, :, D + 1], 0.0))
            st["wd"] = dve.do(lambda e: e.tensor_scalar(wd[:, :, 0:D], wd[:, :, 0:D], -2.0, None, ALU.mult),
                              st["bT"])
            for c in range(2):
                a = mm(pX[0:1, 0:8], ones[:, 0:1], bTq[:, c, :], st["bTq"], last["pX"], start=c == 0,
                       stop=c == 1, inc=c == 1)
            a = dve.do(lambda e: e.tensor_scalar(trow[:, :], pX[0:1, 0:8], float(T), None, ALU.mult), a)
            last["pX"] = a
            st["trow"] = a

        def setup_c():
            for p in range(4):
                for c in range(2):
                    w = wdT_s[:, c, 128 * p:128 * p + 128]
                    a = mm(pX[:, 128 * p:128 * p + 128], w, w, last["pX"], st["w"][1], start=c == 0,
                           stop=c == 1, inc=c == 1)
            st["setup"] = a
            for k in range(2):
                a = dve.do(lambda e, k=k: e.tensor_scalar(
                    ww[:, :, 64 * k:64 * k + 64], pX[:, :].rearrange("p (a b) -> p a b", a=4)[:, :, 64 * k:64 * k + 64],
                    bmask[:, k:k + 1], None, ALU.mult), a)
            last["pX"] = a
            st["ww"] = a

        plan = {}

        def at(U, *fs):
            plan.setdefault(U, []).extend(fs)

        def ln1_at(b, k, U):
            at(U, ln1_load(b, k))
            at(U + 2, ln1_stats(b, k))
            at(U + 3, ln1_norm(b, k))
            at(U + 4, ln1_turn(b, k))

        for b in range(NB + 1):
            B = UB * b
            if b < NB:
                at(B + 0, qk_group(b, 1, 0, 0))
                at(B + 1, qk_group(b, 1, 0, 1))
                at(B + 10, qk_group(b, 1, 1, 0))
                at(B + 11, qk_group(b, 1, 1, 1))
            if b >= 1:
                q = b - 1
                at(B + 2, at_turn(q, 0), at_turn(q, 1))
                at(B + 3, at_turn(q, 2), at_turn(q, 3))
                for k in range(4):
                    at(B + 4 + k, proj(q, k))
                at(B + 8, ln2_stats(q))
                for k in range(4):
                    at(B + 9 + k, ln2_norm(q, k))
                for k in range(4):
                    at(B + 12 + k, x_turn(q, k))
                for t in range(8):
                    at(B + 16 + t, enc(q, t))
                for p in range(4):
                    at(B + 24 + 4 * p, gram_c(q, p))
                    at(B + 26 + 4 * p, gram_a(q, p))
                at(B + 40, select(q))
                at(B + 41, fetch(q))
                for h in range(2):
                    at(B + 45 + 4 * h, mid_mm(q, h))
                    at(B + 46 + 4 * h, out_mm(q, 2 * h))
                    at(B + 47 + 4 * h, out_mm(q, 2 * h + 1))
            if b < NB:
                at(B + 56, prep(b))
            if b == 0:
                at(2, setup_a)
                at(4, setup_b)
                at(6, setup_c)
            if b + 1 < NB:
                for k in range(4):
                    ln1_at(b + 1, k, B + 12 + 5 * k)
                at(B + 33, qk_group(b + 1, 0, 0, 0))
                at(B + 34, qk_group(b + 1, 0, 0, 1))
                at(B + 42, qk_group(b + 1, 0, 1, 0))
                at(B + 43, qk_group(b + 1, 0, 1, 1))
                for k in range(4):
                    at(B + 53 + k, v_group(b + 1, k))

        for k in range(4):
            for f in (ln1_load, ln1_stats, ln1_norm, ln1_turn):
                f(0, k)()
        for w in range(2):
            for half in range(2):
                qk_group(0, 0, w, half)()
        for k in range(4):
            v_group(0, k)()
        st["w"] = load_ffn_weights()
        n_m = 32 * NB * 4
        m_next = 0

        def m_some(n):
            nonlocal m_next
            for _ in range(n):
                if m_next < n_m:
                    m_tile(m_next)
                    m_next += 1
        m_some(16)
        m_turn(0)
        m_some(2 * LA)

        NU = UB * NB
        for U in range(NU):
            m_due = (U + LA) // 8 + 1
            e_tile(U, 0)
            e_tile(U, 1)
            m_some(1)
            e_tile(U, 2)
            m_some(1)
            e_tile(U, 3)
            if (U + LA) % 8 == 7 and m_due < 2 * 4 * NB:
                m_turn(m_due)
            if U:
                pv(U - 1)
                if (U - 1) % 8 == 7:
                    st["o"] = U - 1
            if U % 8 == 1 and "o" in st:
                o_turn(st.pop("o"))
            for f in plan.get(U, ()):
                f()
        pv(NU - 1)
        o_turn(NU - 1)
        for U in sorted(k for k in plan if k >= NU):
            for f in plan[U]:
                f()
        sp.do(lambda e: None, st["x2_out"], ev_modd, inc=False)

        block = ctx.enter_context(nc.Block())

        @block.sync
        def _(e):
            sp.emit(e)

        @block.tensor
        def _(e):
            pe.emit(e)

        @block.vector
        def _(e):
            dve.emit(e)

        @block.scalar
        def _(e):
            act.emit(e)

        @block.gpsimd
        def _(e):
            pool.emit(e)


def kernel(**inputs):
    import numpy as np
    import concourse.bacc as bacc
    from concourse.bass_utils import run_bass_kernel_spmd as run

    g = {k: np.asarray(v) for k, v in inputs.items()}
    p = "L0_ffn_"
    consts = np.zeros((128, 138), np.float32)
    consts[:, 0:128] = np.eye(128)
    consts[:64, 128] = 1
    consts[64:, 129] = 1
    consts[:, 130:138] = np.arange(8)
    wenc = g[p + "W_enc"].transpose(1, 0, 2).reshape(D, NE * H)
    wdec = g[p + "W_dec"].reshape(NE * H, D)
    benc = g[p + "b_enc"].reshape(1, NE * H)
    arrays = [
        ("x", g["L0_attn_x"]), ("wqkvT", g["L0_attn_qkv_w"].T), ("wpT", g["L0_attn_proj_w"].T),
        ("pb", g["L0_attn_proj_b"].reshape(1, D)), ("wbase", g[p + "W_base"]),
        ("bbase", g[p + "b_base"].reshape(1, D)), ("wenc", wenc), ("benc", benc),
        ("bencc", benc.reshape(4, 128).T), ("wdec", wdec), ("wdecT", wdec.T), ("bdecT", g[p + "b_dec"].T),
        ("wdown", g[p + "W_down"]), ("bdown", g[p + "b_down"]), ("wup", g[p + "W_up"]),
        ("bup", g[p + "b_up"]), ("cidx", g[p + "connected_idx"].reshape(1, NE)),
        ("cT", g["L0_c"].T), ("wmod", g["L0_wmod"]), ("consts", consts),
    ]
    arrays = {f"in_{n}": np.ascontiguousarray(a) for n, a in arrays}
    nc = bacc.Bacc("TRN2", target_bir_lowering=False, num_devices=1)
    args = [nc.dram_tensor(n, a.shape, mybir.dt.from_np(a.dtype), kind="ExternalInput").ap()
            for n, a in arrays.items()]
    out = nc.dram_tensor("out_0", (NB, T, D), F, kind="ExternalOutput").ap()
    adaln_block(nc, *args, out)
    r = run(nc, [arrays], core_ids=[0])
    return r.results[0]["out_0"]
```

```python
from contextlib import ExitStack

import concourse.bass as bass
from concourse import mybir

F = mybir.dt.float32
R = mybir.dt.float32r
I32 = mybir.dt.int32
U32 = mybir.dt.uint32
ACT = mybir.ActivationFunctionType
ALU = mybir.AluOpType
AX = mybir.AxisListType

NB, T, D = 4, 1024, 256
NH, HD = 16, 16
NE, H = 8, 64
QC = 48
QM = QC + 2
NEB = 3
LA = 4
MD = 1
MV = 1
MJ = 2
UB = 64
EPS = 1e-5


class Queue:

    def __init__(self, sem):
        self.sem, self.n, self.ops = sem, 0, []

    def do(self, fn, *after, inc=True):
        self.n += inc
        self.ops.append((after, fn, self.sem if inc else None))
        return (self.sem, self.n)

    def emit(self, eng):
        seen = {}
        for after, fn, sem in self.ops:
            for s, n in after:
                if seen.get(id(s), 0) < n:
                    eng.wait_ge(s, n)
                    seen[id(s)] = n
            ins = fn(eng)
            if sem is not None:
                ins.then_inc(sem, 1)


class Landing:

    def __init__(self, sem):
        self.sem, self.n = sem, 0

    def ev(self):
        return (self.sem, self.n)


def adaln_block(nc, x, wqkvT, wpT, pb, wbase, bbase, wenc, benc, bencc, wdec, wdecT, bdecT,
                wdown, bdown, wup, bup, cidx, cT, wmod, consts, out):
    ctx = ExitStack()
    with ctx:
        def sb(name, shape, dt=F):
            return ctx.enter_context(nc.sbuf_tensor(name, shape, dt))

        def sem(name):
            return ctx.enter_context(nc.semaphore(name))

        pM = ctx.enter_context(nc.psum_tensor("pM", [128, 2, 512], F))
        pE = ctx.enter_context(nc.psum_tensor("pE", [128, NEB, 512], F))
        pO = ctx.enter_context(nc.psum_tensor("pO", [128, 512], F))
        pX = ctx.enter_context(nc.psum_tensor("pX", [128, 5 - NEB, 512], F))
        modd = nc.dram_tensor("modd", [NB, 6 * D], F, kind="Internal").ap()

        QO = sb("QO", [128, 2, 4, T], R)
        KO = sb("KO", [128, 2, 4, T], R)
        V = sb("V", [128, 2, 8, NH, HD + 1])
        P = sb("P", [128, 2, 4, 512])
        hi = sb("hi", [128, T], R)
        lo = sb("lo", [128, T], R)
        osb = sb("osb", [128, 512])
        Atok = sb("Atok", [128, 8, D])
        xin = sb("xin", [128, 2, D])
        h1T = sb("h1T", [128, 2, T])
        h2T = sb("h2T", [128, 2, T])
        x2 = sb("x2", [128, 8, D])
        X = sb("X", [128, 8, D + 2])
        Hb = sb("Hb", [128, 8, 512])
        mid = sb("mid", [128, 512])
        wqkv_s = sb("wqkv_s", [128, 2, 3 * D])
        wp_s = sb("wp_s", [128, 2, D])
        wpg = sb("wpg", [128, 2, D])
        wb_s = sb("wb_s", [128, 2, D])
        wbg = sb("wbg", [128, 2, D])
        wenc_s = sb("wenc_s", [128, 2, 512])
        wd = sb("wd", [128, 4, D + 2])
        ww = sb("ww", [128, 4, 128])
        wdn = sb("wdn", [128, 2, H])
        bdn = sb("bdn", [H, 1])
        wug = sb("wug", [H + 1, D])
        bbr = sb("bbr", [H + 1, D])
        bc = sb("bc", [128, 4, D])
        pbb = sb("pbb", [128, D])
        nbe = sb("nbe", [128, 512])
        cst = sb("cst", [128, 138])
        cT_s = sb("cT_s", [128, 2, NB])
        sg = sb("sg", [128, 3, 2 * NB])
        modT = sb("modT", [128, 4, NB])
        ones = sb("ones", [128, 8])
        st1 = sb("st1", [128, 2, 6])
        mv1 = sb("mv1", [128, 2, 2])
        rs1 = sb("rs1", [128, 2, 2])
        st2 = sb("st2", [128, 8, 6])
        mv2 = sb("mv2", [128, 8, 2])
        rs2 = sb("rs2", [128, 2, 8])
        nh = sb("nh", [128, 8])
        mx = sb("mx", [128, 2, 16, 2])
        mxc = sb("mxc", [128, 16])
        mhl = sb("mhl", [128, 2, 32])
        mh = sb("mh", [128, 16], R)
        mT = sb("mT", [32, 2, 128])
        rec = sb("rec", [128, 4, 4])
        junk = sb("junk", [128, 258])
        junk2 = sb("junk2", [128, 256])
        accC = sb("accC", [128, 4])
        accA = sb("accA", [128, 4])
        ps = sb("ps", [128, 4])
        pl8 = sb("pl8", [128, 4, 2])
        xsq = sb("xsq", [128, 8])
        xsq1 = sb("xsq1", [128, 1])
        xbar = sb("xbar", [128, 2, 2])
        bT = sb("bT", [128, 2, 8])
        bTm = sb("bTm", [128, 2, 8])
        bTq = sb("bTq", [128, 2, 8])
        be = sb("be", [128, 4, 8])
        bec = sb("bec", [128, 4])
        bdT = sb("bdT", [128, 2, 8])
        trow = sb("trow", [1, 8])
        connf = sb("connf", [1, 8])
        conni = sb("conni", [1, 8], I32)
        sel = sb("sel", [1, 8, 8])
        selu = sb("selu", [1, 8], U32)
        seli = sb("seli", [1, 1], I32)

        ident = cst[:, 0:128]
        bmask = cst[:, 128:130]
        iota8 = cst[0:1, 130:138]
        wmod_s = Hb[:, 0:6, :].rearrange("p a b -> p (a b)").rearrange("p (c n) -> p c n", c=2)
        wdT_s = Hb[:, 6:8, :]
        AT = Hb[:, 0:4, :].rearrange("p a b -> p (a b)").rearrange("p (c n) -> p c n", c=2)
        gt = Atok[0:NB, 0:4, :].rearrange("p (a b) n -> p a b n", a=2)
        modr = X[0:NB, :, :].rearrange("p a b -> p (a b)")

        pe, act, dve, pool = (Queue(sem(n)) for n in ("s_pe", "s_act", "s_dve", "s_pool"))
        sp = Queue(None)
        places = {}

        def dma(place, dst, src, *after):
            if place not in places:
                places[place] = Landing(sem("d_" + place))
            p = places[place]
            p.n += 16
            sp.do(lambda e: e.dma_start(dst, src).then_inc(p.sem, 16), *after, inc=False)
            return p.ev()

        class Bank:

            def __init__(self, t):
                self.t, self.ev, self.held, self.at = t, None, False, 0

            def free(self, ev):
                self.ev, self.held = ev, False

        banks = [Bank(pX[:, i, :]) for i in range(5 - NEB)]
        spare = [Bank(pM[:, i, :]) for i in range(2)] + [Bank(pE[:, i, :]) for i in range(NEB)]
        turn = [0]

        use = {"banks": banks + spare}

        def grab():
            bk = min((x for x in use["banks"] if not x.held), key=lambda x: x.at)
            turn[0] += 1
            bk.held, bk.at = True, turn[0]
            return bk

        def mm(outp, lhsT, rhs, *after, start=True, stop=True, inc=True, skip=False):
            return pe.do(lambda e: e.matmul(outp, lhsT, rhs, start=start, stop=stop,
                                            skip_group_check=skip), *after, inc=inc)

        def tr(outp, in_, idn, *after, inc=True):
            return pe.do(lambda e: e.transpose(outp, in_, idn), *after, inc=inc)

        ev_cst = dma("cst", cst[:, :], consts)
        ev_cT = dma("cT", cT_s[:, :, :], cT.rearrange("(c p) b -> p c b", p=128))
        x_tiles = x.rearrange("b (t p) d -> b p t d", p=128)
        ev_xin = dma("xin", xin[:, :, :], x_tiles[0, :, 0:2, :])
        ev_wmod = dma("wmod", wmod_s, wmod.rearrange("(c p) n -> p c n", p=128))
        ev_wqkv = dma("wqkv", wqkv_s[:, :, :], wqkvT.rearrange("(c p) n -> p c n", p=128))

        def load_ffn_weights():
            evs = [
                dma("w0", wd[:, :, 0:D], wdec.rearrange("(c p) n -> p c n", p=128)),
                dma("w1", wdT_s, wdecT.rearrange("(c p) n -> p c n", p=128)),
                dma("w2", bec[:, :], bencc),
                dma("w3", bdT[:, :, :], bdecT.rearrange("(c p) n -> p c n", p=128)),
                dma("w4", wp_s[:, :, :], wpT.rearrange("(c p) n -> p c n", p=128)),
                dma("w5", wb_s[:, :, :], wbase.rearrange("(c p) n -> p c n", p=128)),
                dma("w6", wenc_s[:, :, :], wenc.rearrange("(c p) n -> p c n", p=128)),
                dma("w7", pbb[:, :], pb.to_broadcast([128, D])),
                dma("w8", nbe[:, :], benc.to_broadcast([128, 512])),
                dma("w9", bbr[H:H + 1, :], bbase),
                dma("w10", conni[:, :], cidx),
            ]
            return evs

        ev_ones = pool.do(lambda e: e.memset(ones[:, :], 1.0))
        ev_nh = pool.do(lambda e: e.memset(nh[:, :], -0.5))
        ev_vone = pool.do(lambda e: e.memset(V[:, :, :, :, HD:], 1.0))
        ev_mid1 = dve.do(lambda e: e.memset(mid[H:H + 1, :], 1.0))
        pf = P[0:2, :, :, :].rearrange("p a b n -> p (a b n)")
        ev_pone = pool.do(lambda e: e.memset(pf, 1.0), ev_vone)
        for half in (0, 1):
            for slot in (0, 1):
                ev_kone = dma("kone", KO[64 * half + QC:64 * half + QM, slot, :, :].bitcast(F), pf, ev_pone)

        ev_po = dve.do(lambda e: e.memset(pO[:, :], 0.0))

        c8 = cT_s[:, :, :].rearrange("p a b -> p (a b)")
        e1 = act.do(lambda e: e.activation(sg[:, 0, :], c8, ACT.Exp, scale=-1.0), ev_cT)
        e2 = dve.do(lambda e: e.tensor_scalar(sg[:, 1, :], sg[:, 0, :], 1.0, None, ALU.add), e1)
        e3 = dve.do(lambda e: e.reciprocal(sg[:, 2, :], sg[:, 1, :]), e2)
        e4 = dve.do(lambda e: e.tensor_tensor(sg[:, 0, :], sg[:, 2, :], c8, ALU.mult), e3)
        mod_ev = []
        for j in range(3):
            bk = grab()
            for c in range(2):
                ev = mm(bk.t[0:NB, :], sg[:, 0, NB * c:NB * c + NB],
                        wmod_s[:, c, 512 * j:512 * j + 512], e4, ev_wmod, start=c == 0, stop=c == 1,
                        inc=c == 1)
            mod_ev.append(act.do(lambda e, j=j, bk=bk: e.activation(modr[:, 512 * j:512 * j + 512],
                                                                    bk.t[0:NB, :], ACT.Copy), ev))
            bk.free(mod_ev[-1])
        evc = dve.do(lambda e: e.tensor_scalar(modr[:, 256:512], modr[:, 256:512], 1.0, None, ALU.add), mod_ev[0])
        evb = dve.do(lambda e: e.tensor_scalar(modr[:, 1024:1280], modr[:, 1024:1280], 1.0, None, ALU.add),
                     mod_ev[2])
        evg = []
        for k, o in ((0, 512), (1, 1280)):
            a = dve.do(lambda e, k=k, o=o: e.tensor_scalar(gt[:, k, 0, :], modr[:, o:o + 256], 0.0, 2.0,
                                                           ALU.is_ge, ALU.mult), mod_ev[2])
            a = dve.do(lambda e, k=k, o=o: e.scalar_tensor_tensor(
                out=gt[:, k, 1, :], in0=modr[:, o:o + 256], scalar=-1.0, in1=modr[:, o:o + 256],
                op0=ALU.mult, op1=ALU.max))
            a = dve.do(lambda e, k=k: e.tensor_scalar(gt[:, k, 1, :], gt[:, k, 1, :], 0.25, None, ALU.max), a)
            evg.append(dve.do(lambda e, k=k, o=o: e.scalar_tensor_tensor(
                out=modr[:, o:o + 256], in0=gt[:, k, 0, :], scalar=-1.0, in1=gt[:, k, 1, :],
                op0=ALU.add, op1=ALU.mult), a))
        ev_modd = dma("modd", modd, modr[:, 0:6 * D], evc, evb, *evg)
        bk0 = grab()
        for k in range(4):
            evt = tr(bk0.t[:, NB * k:NB * k + NB], modr[:, 128 * k:128 * k + 128], ident[0:NB, 0:NB],
                     evc, ev_cst, inc=k == 3)
        ev_modT = dve.do(lambda e: e.tensor_copy(modT[:, :, :].rearrange("p a b -> p (a b)"), bk0.t[:, 0:16]), evt)
        bk0.free(ev_modT)

        last = {"P": [ev_kone] * 2, "M": None, "pO": ev_po,
                "hilo_in": None, "xin": ev_xin}

        def after(*evs):
            return [e for e in evs if e is not None]

        h1_ready = [[None] * 4 for _ in range(NB)]
        h1_read = [None]
        xin_free = [None]

        def ln1_load(b, k):
            def f():
                if (b, k) != (0, 0):
                    last["xin"] = dma("xin", xin[:, :, :], x_tiles[b, :, 2 * k:2 * k + 2, :],
                                      *after(xin_free[0]))
            return f

        def ln1_stats(b, k):
            def f():
                for t in range(2):
                    a = dve.do(lambda e, t=t: e.bn_stats(st1[:, t, :], xin[:, t, :]), last["xin"])
                    if t == 0:
                        yield
                for t in range(2):
                    a = dve.do(lambda e, t=t: e.bn_aggr(mv1[:, t, :], st1[:, t, :]), a)
                a = pool.do(lambda e: e.tensor_scalar(rs1[:, 0, :], mv1[:, :, 1], EPS, None, ALU.add), a, ev_pone)
                a = pool.do(lambda e: e.tensor_tensor(rs1[:, 1, :], rs1[:, 0, :], nh[:, 0:2], ALU.pow), a)
                last["rs1"] = a
            return f

        def ln1_norm(b, k):
            def f():
                for t in range(2):
                    last["xn"] = pool.do(lambda e, t=t: e.tensor_scalar(
                        xin[:, t, :], xin[:, t, :], mv1[:, t, 0:1], rs1[:, 1, t:t + 1], ALU.subtract,
                        ALU.mult), last["rs1"])
            return f

        def ln1_turn(b, k):
            def f():
                bk = grab()
                for c in range(2):
                    for t in range(2):
                        a = tr(bk.t[:, 256 * c + 128 * t:256 * c + 128 * t + 128],
                               xin[:, t, 128 * c:128 * c + 128], ident, last["xn"], *after(bk.ev),
                               inc=c == 1 and t == 1)
                xin_free[0] = a
                for c in range(2):
                    g = act.do(lambda e, c=c: e.activation(
                        h1T[:, c, 256 * k:256 * k + 256], bk.t[:, 256 * c:256 * c + 256], ACT.Identity,
                        bias=modT[:, c, b:b + 1], scale=modT[:, 2 + c, b:b + 1]),
                        *after(a, ev_modT, h1_read[0]))
                bk.free(g)
                h1_ready[b][k] = g
            return f

        oct_ready = {}
        moving = []

        def move(n):
            for _ in range(n):
                while moving:
                    try:
                        next(moving[0])
                        break
                    except StopIteration:
                        moving.pop(0)

        e_done = {}

        def qk_group(b, o, w, half):
            def f():
                bk = grab()
                r0 = 256 * w + 128 * o
                for c in range(2):
                    a = mm(bk.t[:, :], wqkv_s[:, c, r0:r0 + 128], h1T[:, c, 512 * half:512 * half + 512],
                           ev_wqkv, *after(bk.ev), h1_ready[b][2 * half + 1], start=c == 0, stop=c == 1,
                           inc=c == 1)
                    if c == 0:
                        yield
                h1_read[0] = a
                cs = slice(512 * half, 512 * half + 512)
                sc = 0.25 if w == 0 else 1.0
                a = act.do(lambda e: e.activation(hi[:, cs], bk.t[:, :], ACT.Copy, scale=sc),
                           *after(a, last["hilo_in"]))
                a = dve.do(lambda e: e.scalar_tensor_tensor(out=lo[:, cs], in0=bk.t[:, :], scalar=sc,
                                                            in1=hi[:, cs].bitcast(F), op0=ALU.mult,
                                                            op1=ALU.subtract), a)
                bk.free(a)
                if half == 1:
                    slot = (2 * b + o) % 2
                    dst = KO if w else QO
                    parts = (hi, lo, hi) if w else (hi, hi, lo)
                    n = 2 * b + o
                    evs = after(a, ev_kone, e_done.get(n - 2))

                    def copies():
                        for h in range(8):
                            for r in range(3):
                                p0 = 64 * (h % 2) + 16 * r
                                ev = dma(f"op{w}{slot}", dst[p0:p0 + 16, slot, h // 2, :].bitcast(F),
                                         parts[r][16 * h:16 * h + 16, :].bitcast(F), *evs)
                                if h == 7 and r == 2:
                                    last["hilo_in"] = ev
                                    oct_ready[(n, w)] = ev
                                yield
                    moving.append(copies())
            return f

        v_ready = {}
        pv_done = {}

        def v_group(b, k):
            def f():
                bk = grab()
                for t in range(2):
                    for c in range(2):
                        tt = 2 * k + t
                        a = mm(bk.t[:, 256 * t:256 * t + 256], h1T[:, c, 128 * tt:128 * tt + 128],
                               wqkv_s[:, c, 512:768], ev_wqkv, *after(bk.ev), h1_ready[b][k],
                               start=c == 0, stop=c == 1, inc=c == 1 and t == 1)
                    if t == 0:
                        yield
                h1_read[0] = a
                a = act.do(lambda e: e.activation(V[:, b % 2, 2 * k:2 * k + 2, :, 0:HD],
                                                  bk.t[:, :].rearrange("p (t h e) -> p t h e", t=2, e=HD), ACT.Copy),
                           *after(a, pv_done.get(b - 2)))
                bk.free(a)
                v_ready[(b, k)] = a
            return f

        m_last = {}
        m_rows = {}
        mx_free = [None, None]

        def operand(buf, gi, j, rows, sl):
            base = 64 * (j % 2)
            return buf[base:base + rows, (gi // 2) % 2, 2 * (gi % 2) + j // 2, sl]

        def m_tile(i):
            hq, k = divmod(i, 32)
            gi, c = divmod(hq, 2)
            k, kh = divmod(k, 2)
            j, qb = divmod(k, 4)
            s = i % 2
            q0 = 512 * c + 128 * qb
            n = gi // 2
            a = mm(pM[:, s, :], operand(QO, gi, j, QC, slice(q0, q0 + 128)),
                   operand(KO, gi, j, QC, slice(512 * kh, 512 * kh + 512)), *after(last["M"][s]),
                   oct_ready[(n, 0)], oct_ready[(n, 1)])
            g = dve.do(lambda e: e.tensor_reduce(mx[:, hq % 2, k:k + 1, kh], pM[:, s, :], AX.X, ALU.max,
                                                 negate=True), *after(a, mx_free[hq % 2]))
            last["M"][s] = g
            if i % 32 == 31:
                v = mx[:, hq % 2, :, :]
                a = dve.do(lambda e: e.tensor_tensor(mxc[:, :], v[:, :, 0], v[:, :, 1], ALU.min), g)
                a = dve.do(lambda e: e.tensor_copy(mh[:, :], mxc[:, :]), a)
                dve.do(lambda e: e.tensor_copy(mhl[:, hq % 2, 0:16], mh[:, :].bitcast(F)), a)
                m_last[hq] = dve.do(lambda e: e.tensor_tensor(mhl[:, hq % 2, 16:32], mxc[:, :],
                                                              mh[:, :].bitcast(F), ALU.subtract), a)
                mx_free[hq % 2] = m_last[hq]

        def m_turn(hq):
            bk = grab()
            gi, c = divmod(hq, 2)
            a = tr(bk.t[0:32, 0:128], mhl[:, hq % 2, :], ident, m_last[hq], *after(bk.ev))
            mx_free[hq % 2] = a
            a = act.do(lambda e: e.activation(mT[:, hq % 2, :], bk.t[0:32, 0:128], ACT.Copy),
                       *after(a, m_rows.get(hq - 2)))
            bk.free(a)
            for r in range(2):
                for j in range(4):
                    p0 = 64 * (j % 2) + QC + r
                    dst = QO[p0:p0 + 1, (gi // 2) % 2, 2 * (gi % 2) + j // 2, 512 * c:512 * c + 512]
                    ev = dma(f"m{hq % 2}", dst.rearrange("p (a b) -> p a b", a=4).bitcast(F),
                             mT[16 * r + 4 * j:16 * r + 4 * j + 4, hq % 2, :], a)
            m_rows[hq] = ev

        e_count = [0]
        exp_ev = {}

        def e_tile(U, j):
            gi, u = divmod(U, 16)
            c, kb = divmod(u, 8)
            s = e_count[0] % NEB
            e_count[0] += 1
            a = mm(pE[:, s, :], operand(KO, gi, j, QM, slice(128 * kb, 128 * kb + 128)),
                   operand(QO, gi, j, QM, slice(512 * c, 512 * c + 512)),
                   *after(m_rows[2 * gi + c], last["E"][s], oct_ready[(gi // 2, 0)], oct_ready[(gi // 2, 1)]))
            e_done[gi // 2] = a
            g = act.do(lambda e: e.activation(P[:, U % 2, j, :], pE[:, s, :], ACT.Exp),
                       *after(a, last["P"][U % 2]))
            last["E"][s] = g
            exp_ev[U] = g

        def pv(U):
            gi, u = divmod(U, 16)
            kb = u % 8
            b = gi // 4
            for j in range(4):
                h = 4 * (gi % 4) + j
                a = mm(pO[32 * j:32 * j + HD + 1, :], V[:, b % 2, kb, h, :], P[:, U % 2, j, :],
                       *after(exp_ev[U], v_ready[(b, kb // 2)], ev_vone, last["pO"] if kb == 0 else None),
                       start=kb == 0, stop=kb == 7, inc=j == 3)
            last["P"][U % 2] = a
            pv_done[b] = a
            if kb == 7:
                a = act.do(lambda e: e.activation(osb[:, :], pO[:, :], ACT.Copy), *after(a, last.get("osb")))
                last["pO"] = a
                last["osb_in"] = a

        at_ev = {}

        def o_turn(U):
            bk = grab()
            gi, u = divmod(U, 16)
            c, b, g = u // 8, gi // 4, gi % 4
            for k in range(4):
                a = tr(bk.t[:, 128 * k:128 * k + 128], osb[:, 128 * k:128 * k + 128], ident,
                       last["osb_in"], *after(bk.ev), inc=k == 3)
            last["osb"] = a
            v = bk.t[:, :].rearrange("p (k j e) -> p k j e", k=4, j=4)
            a = dve.do(lambda e: e.reciprocal(rec[:, :, :], v[:, :, :, HD]), a)
            dst = Atok[:, 4 * c:4 * c + 4, 64 * g:64 * g + 64].rearrange("p k (j e) -> p k j e", j=4)
            a = dve.do(lambda e: e.tensor_tensor(
                dst, v[:, :, :, 0:HD], rec[:, :, :].unsqueeze(3).to_broadcast([128, 4, 4, HD]), ALU.mult),
                *after(a, at_ev.get((b - 1, 3))))
            bk.free(a)
            last["Atok"] = a

        st = {}

        def at_turn(b, k):
            def f():
                bk = grab()
                c, th = k // 2, k % 2
                for t in range(4):
                    a = tr(bk.t[:, 128 * t:128 * t + 128], Atok[:, 4 * th + t, 128 * c:128 * c + 128], ident,
                           last["Atok"], *after(bk.ev), inc=t == 3)
                at_ev[(b, k)] = a
                a = act.do(lambda e: e.activation(AT[:, c, 512 * th:512 * th + 512], bk.t[:, :], ACT.Copy),
                           *after(a, st.get("Hread"), st.get("setup")))
                bk.free(a)
                st["AT"] = a
            return f

        def prep(b):
            def f():
                for k, o in enumerate((512, 768, 1024, 1280)):
                    st["bc"] = dma("bc", bc[:, k, :], modd[b:b + 1, o:o + 256].to_broadcast([128, 256]),
                                   *after(ev_modd, st.get("bc_read")))
                ev = dma("x2", x2[:, :, :], x_tiles[b], *after(st.get("x2_out")))
                ga = bc[:, 0:1, :].to_broadcast([128, 2, D])
                gb = bc[:, 3:4, :].to_broadcast([128, 2, D])
                a = pool.do(lambda e: e.tensor_tensor(wpg[:, :, :], wp_s[:, :, :], ga, ALU.mult),
                            *after(st["bc"], st["w"][4], st.get("proj")))
                a = pool.do(lambda e: e.tensor_tensor(bc[:, 0, :], pbb[:, :], bc[:, 0, :], ALU.mult), a,
                            st["w"][7])
                pool.do(lambda e: e.tensor_tensor(wbg[:, :, :], wb_s[:, :, :], gb, ALU.mult), st["w"][5],
                        *after(st.get("outmm")))
                for t in range(8):
                    st["x2"] = pool.do(lambda e, t=t: e.tensor_tensor(x2[:, t, :], x2[:, t, :], bc[:, 0, :],
                                                                      ALU.add), ev, a)
            return f

        def proj(b, k):
            def f():
                bk = grab()
                for t in range(2):
                    for c in range(2):
                        tt = 2 * k + t
                        a = mm(bk.t[:, 256 * t:256 * t + 256], AT[:, c, 128 * tt:128 * tt + 128], wpg[:, c, :],
                               st["AT"], st["x2"], *after(bk.ev), start=c == 0, stop=c == 1,
                               inc=c == 1 and t == 1)
                    if t == 0:
                        yield
                st["proj"] = a
                sl = x2[:, 2 * k:2 * k + 2, :]
                a = dve.do(lambda e: e.tensor_tensor(sl, bk.t[:, :].rearrange("p (t n) -> p t n", t=2), sl,
                                                     ALU.add), a)
                bk.free(a)
                for t in range(2):
                    yield
                    st["st2"] = dve.do(lambda e, t=t: e.bn_stats(st2[:, 2 * k + t, :], x2[:, 2 * k + t, :]), a)
            return f

        def ln2_stats(b):
            def f():
                a = st["st2"]
                for t in range(8):
                    a2 = dve.do(lambda e, t=t: e.bn_aggr(mv2[:, t, :], st2[:, t, :]), a)
                a = pool.do(lambda e: e.tensor_scalar(rs2[:, 0, :], mv2[:, :, 1], EPS, None, ALU.add), a2)
                st["rs2"] = pool.do(lambda e: e.tensor_tensor(rs2[:, 1, :], rs2[:, 0, :], nh[:, :], ALU.pow), a)
                if b == 0:
                    st["xone"] = pool.do(lambda e: e.memset(X[:, :, D:D + 2], 1.0), ev_modd, evt)
            return f

        def ln2_norm(b, k):
            def f():
                evs = []
                for t in (2 * k, 2 * k + 1):
                    if t % 2:
                        yield
                    evs.append(dve.do(lambda e, t=t: e.scalar_tensor_tensor(
                        out=X[:, t, 0:D], in0=x2[:, t, :], scalar=mv2[:, t, 0:1], in1=bc[:, 2, :],
                        op0=ALU.subtract, op1=ALU.mult), *after(st["rs2"], st["bc"], st.get("Xread"), ev_modd, evt)))
                for i, t in enumerate((2 * k, 2 * k + 1)):
                    yield
                    a = dve.do(lambda e, t=t: e.scalar_tensor_tensor(
                        out=X[:, t, 0:D], in0=X[:, t, 0:D], scalar=rs2[:, 1, t:t + 1], in1=bc[:, 1, :],
                        op0=ALU.mult, op1=ALU.add), evs[i])
                st[("X", k)] = a
                for t in (2 * k, 2 * k + 1):
                    yield
                    g = act.do(lambda e, t=t: e.activation(junk2[:, :], X[:, t, 0:D], ACT.Square,
                                                           accum_out=xsq[:, t:t + 1]),
                               *after(a, st.get("xsq"), st.get("xsq_read")))
                    st["xsq"] = g
            return f

        def x_turn(b, k):
            def f():
                bk = grab()
                c, th = k % 2, k // 2
                for t in range(4):
                    a = tr(bk.t[:, 128 * t:128 * t + 128], X[:, 4 * th + t, 128 * c:128 * c + 128], ident,
                           st[("X", 2 * th + t // 2)], *after(bk.ev), inc=t == 3)
                a = act.do(lambda e: e.activation(h2T[:, c, 512 * th:512 * th + 512], bk.t[:, :], ACT.Identity,
                                                  accum_out=xbar[:, c, th:th + 1]),
                           *after(a, st.get("outmm"), st.get("Lmm")))
                bk.free(a)
                st[("h2T", th)] = a
            return f

        def enc(b, t):
            def f():
                bk = grab()
                for c in range(2):
                    a = mm(bk.t[:, :], h2T[:, c, 128 * t:128 * t + 128], wenc_s[:, c, :], st[("h2T", t // 4)],
                           st["w"][6], *after(bk.ev), start=c == 0, stop=c == 1, inc=c == 1)
                    if c == 0:
                        yield
                a = dve.do(lambda e: e.tensor_tensor(Hb[:, t, :], bk.t[:, :], nbe[:, :], ALU.max),
                           *after(a, st["nbe"], st["proj"], st.get("Hread")))
                bk.free(a)
                st["H"] = a
            return f

        def gram_c(b, p):
            def f():
                bk = grab()
                for t in range(8):
                    a = mm(bk.t[:, 0:D + 2], Hb[:, t, 128 * p:128 * p + 128], X[:, t, :], st["H"], *after(bk.ev),
                           st["xone"], start=t == 0, stop=t == 7, inc=t == 7)
                    if t in (1, 3, 5):
                        yield
                st["Xread"] = a
                a = dve.do(lambda e: e.tensor_tensor_reduce(junk[:, :], bk.t[:, 0:D + 2], wd[:, p, :], 1.0, 0.0,
                                                            ALU.mult, ALU.add, accC[:, p:p + 1]),
                           *after(a, st["wd"], st.get("junk"), st.get("acc_read")))
                bk.free(a)
                st["junk"] = a
            return f

        def gram_a(b, p):
            def f():
                bk = grab()
                for t in range(8):
                    a = mm(bk.t[:, 0:128], Hb[:, t, 128 * p:128 * p + 128], Hb[:, t, 128 * p:128 * p + 128],
                           st["H"], *after(bk.ev), start=t == 0, stop=t == 7, inc=t == 7)
                    if t == 3:
                        yield
                st["Hread"] = a
                a = dve.do(lambda e: e.tensor_tensor_reduce(junk[:, 0:128], bk.t[:, 0:128], ww[:, p, :], 1.0, 0.0,
                                                            ALU.mult, ALU.add, accA[:, p:p + 1]),
                           *after(a, st["ww"], st.get("junk"), st.get("acc_read")))
                bk.free(a)
                st["junk"] = a
            return f

        def select(b):
            def f():
                a = dve.do(lambda e: e.tensor_tensor(ps[:, :], accC[:, :], accA[:, :], ALU.add),
                           *after(st["junk"], st.get("Lmm")))
                st["acc_read"] = a
                g = dve.do(lambda e: e.tensor_reduce(xsq1[:, :], xsq[:, :], AX.X, ALU.add),
                           *after(st["xsq"], st.get("Lmm")))
                st["xsq_read"] = g
                a = dve.do(lambda e: e.tensor_tensor(
                    pl8[:, :, :], ps[:, :].unsqueeze(2).to_broadcast([128, 4, 2]),
                    bmask.unsqueeze(1).to_broadcast([128, 4, 2]), ALU.mult), a)
                yield
                yield
                yield
                bk = grab()
                L = bk.t[0:1, 0:8]
                mm(L, ones[:, 0:1], pl8[:, :, :].rearrange("p a b -> p (a b)"), a, *after(bk.ev), ev_ones,
                   stop=False, inc=False)
                for c in range(2):
                    for th in range(2):
                        mm(L, xbar[:, c, th:th + 1], bTm[:, c, :], st[("h2T", 0)], st[("h2T", 1)], st["bTm"],
                           start=False, stop=False, inc=False)
                mm(L, xsq1[:, 0:1], ones[:, :], g, start=False, stop=False, inc=False)
                a = mm(L, ones[0:1, 0:1], trow[:, :], st["trow"], start=False)
                st["Lmm"] = a
                a = dve.do(lambda e: e.tensor_scalar(sel[:, 0, :], L, -1.0 / (T * D), None, ALU.mult),
                           *after(a, st.get("seli_read")))
                bk.free(a)
                a = dve.do(lambda e: e.max(sel[:, 1, :], sel[:, 0, :]), a)
                a = dve.do(lambda e: e.max_index(selu[:, :], sel[:, 1, :], sel[:, 0, :]), a)
                a = dve.do(lambda e: e.tensor_copy(sel[:, 2, 0:1], selu[:, 0:1]), a)
                a = dve.do(lambda e: e.tensor_scalar(sel[:, 3, :], iota8, sel[:, 2, 0:1], None, ALU.is_equal), a)
                a = dve.do(lambda e: e.tensor_tensor_reduce(sel[:, 4, :], sel[:, 3, :], connf[:, :], 1.0, 0.0,
                                                            ALU.mult, ALU.add, sel[:, 5, 0:1]),
                           a, st["conn"])
                a = dve.do(lambda e: e.tensor_scalar(sel[:, 5, 1:2], sel[:, 5, 0:1], 0.0, 8.0, ALU.is_lt,
                                                     ALU.mult), a)
                a = dve.do(lambda e: e.tensor_tensor(sel[:, 5, 2:3], sel[:, 5, 0:1], sel[:, 5, 1:2], ALU.add), a)
                a = dve.do(lambda e: e.tensor_scalar(seli[:, :], sel[:, 5, 2:3], 0.0, 7.0, ALU.max, ALU.min), a)
                st["idx"] = a
            return f

        def fetch(b):
            def f():
                vals = {}

                def dyn(place, dst, src, *evs):
                    if place not in places:
                        places[place] = Landing(sem("d_" + place))
                    p = places[place]
                    p.n += 16
                    sp.do(lambda e: e.dma_start(dst, src(vals["v"])).then_inc(p.sem, 16), *evs, inc=False)
                    return p.ev()

                def load(e):
                    vals["v"] = e.value_load(seli[0:1, 0:1], min_val=0, max_val=7)
                sp.do(load, st["idx"], inc=False)
                w = after(st.get("midmm"), st.get("outmm"), st.get("relu"))
                e1 = dyn("sel", wdn[:, :, :], lambda v: wdown[bass.ds(v, 1), :, :].rearrange(
                    "a (c p) r -> p (a c) r", p=128), *w)
                e1 = dyn("sel", bdn[:, :], lambda v: bdown[bass.ds(v, 1), :].rearrange("a r -> r a"))
                e1 = dyn("sel", wug[0:H, :], lambda v: wup[bass.ds(v, 1), :, :].rearrange("a r n -> (a r) n"))
                e1 = dyn("sel", wug[H:H + 1, :], lambda v: bup[bass.ds(v, 1), :])
                st["sel"] = e1
                a = pool.do(lambda e: e.tensor_tensor(wug[H:H + 1, :], wug[H:H + 1, :], bbr[H:H + 1, :],
                                                     ALU.add), e1, st["w"][9])
                a = pool.do(lambda e: e.tensor_tensor(wug[:, :], wug[:, :], bc[0:H + 1, 3, :], ALU.mult), a)
                st["wug"] = a
                st["seli_read"] = e1
                st["bc_read"] = a
            return f

        def mid_mm(b, half):
            def f():
                bk = grab()
                for c in range(2):
                    a = mm(bk.t[0:H, :], wdn[:, c, :], h2T[:, c, 512 * half:512 * half + 512], st["sel"],
                           *after(bk.ev), start=c == 0, stop=c == 1, inc=c == 1)
                    if c == 0:
                        yield
                st["midmm"] = a
                a = act.do(lambda e: e.activation(mid[0:H, :], bk.t[0:H, :], ACT.Relu, bias=bdn[:, 0:1]),
                           *after(a, st.get("outmm")))
                bk.free(a)
                st["mid"] = a
                st["relu"] = a
            return f

        def out_mm(b, k):
            def f():
                bk = grab()
                for t in range(2):
                    tt = 2 * k + t
                    o = bk.t[:, 256 * t:256 * t + 256]
                    for c in range(2):
                        mm(o, h2T[:, c, 128 * tt:128 * tt + 128], wbg[:, c, :], *after(bk.ev), st["x2"],
                           start=c == 0, stop=False, inc=False)
                    m0 = 128 * (tt % 4)
                    a = mm(o, mid[0:H + 1, m0:m0 + 128], wug[:, :], st["mid"], st["wug"], ev_mid1,
                           start=False, inc=t == 1)
                    if t == 0:
                        yield
                st["outmm"] = a
                sl = x2[:, 2 * k:2 * k + 2, :]
                a = dve.do(lambda e: e.tensor_tensor(sl, bk.t[:, :].rearrange("p (t n) -> p t n", t=2), sl,
                                                     ALU.add), a)
                bk.free(a)
                st["x2_out"] = dma("out", out.rearrange("b (t p) d -> b p t d", p=128)[b, :, 2 * k:2 * k + 2, :],
                                   sl, a)
            return f

        def setup_a():
            bk = grab()
            a = dve.do(lambda e: e.memset(be[:, :, :], 0.0))
            for p in range(4):
                g = dve.do(lambda e, p=p: e.tensor_scalar(be[:, p, 2 * p:2 * p + 2], bmask, bec[:, p:p + 1],
                                                          None, ALU.mult), a, st["w"][2], ev_cst)
            for c in range(2):
                for p in range(4):
                    a = mm(bk.t[:, 8 * c:8 * c + 8], wd[:, p, 128 * c:128 * c + 128], be[:, p, :], g,
                           st["w"][0], *after(bk.ev), start=p == 0, stop=p == 3, inc=p == 3)
            a = dve.do(lambda e: e.tensor_tensor(bT[:, :, :], bk.t[:, 0:16].rearrange("p (c n) -> p c n", c=2),
                                                 bdT[:, :, :], ALU.add), a, st["w"][3])
            bk.free(a)
            st["bT"] = a
            st["bTm"] = dve.do(lambda e: e.tensor_scalar(bTm[:, :, :], bT[:, :, :], -2.0, None, ALU.mult), a)
            st["bTq"] = dve.do(lambda e: e.tensor_tensor(bTq[:, :, :], bT[:, :, :], bT[:, :, :], ALU.mult))
            a = dve.do(lambda e: e.tensor_copy(connf[:, :], conni[:, :]), st["w"][10])
            st["conn"] = a
            st["nbe"] = dve.do(lambda e: e.tensor_scalar(nbe[:, :], nbe[:, :], -1.0, None, ALU.mult), st["w"][8])

        def setup_b():
            bk = grab()
            for p in range(4):
                for c in range(2):
                    a = mm(bk.t[:, 8 * p:8 * p + 8], wdT_s[:, c, 128 * p:128 * p + 128], bT[:, c, :], st["bT"],
                           st["w"][1], *after(bk.ev), start=c == 0, stop=c == 1, inc=c == 1)
            for p in range(4):
                g = dve.do(lambda e, p=p: e.scalar_tensor_tensor(
                    out=pl8[:, p, :], in0=bk.t[:, 10 * p:10 * p + 2], scalar=2.0, in1=bmask, op0=ALU.mult,
                    op1=ALU.mult), a)
            bk.free(g)
            g = dve.do(lambda e: e.tensor_reduce(wd[:, :, D], pl8[:, :, :], AX.X, ALU.add), g)
            g = dve.do(lambda e: e.memset(wd[:, :, D + 1], 0.0))
            st["wd"] = dve.do(lambda e: e.tensor_scalar(wd[:, :, 0:D], wd[:, :, 0:D], -2.0, None, ALU.mult),
                              st["bT"])
            bk2 = grab()
            for c in range(2):
                a = mm(bk2.t[0:1, 0:8], ones[:, 0:1], bTq[:, c, :], st["bTq"], *after(bk2.ev), start=c == 0,
                       stop=c == 1, inc=c == 1)
            a = dve.do(lambda e: e.tensor_scalar(trow[:, :], bk2.t[0:1, 0:8], float(T), None, ALU.mult), a)
            bk2.free(a)
            st["trow"] = a

        def setup_c():
            bk = grab()
            for p in range(4):
                for c in range(2):
                    w = wdT_s[:, c, 128 * p:128 * p + 128]
                    a = mm(bk.t[:, 128 * p:128 * p + 128], w, w, *after(bk.ev), st["w"][1], start=c == 0,
                           stop=c == 1, inc=c == 1)
            st["setup"] = a
            for k in range(2):
                a = dve.do(lambda e, k=k: e.tensor_scalar(
                    ww[:, :, 64 * k:64 * k + 64], bk.t[:, :].rearrange("p (a b) -> p a b", a=4)[:, :, 64 * k:64 * k + 64],
                    bmask[:, k:k + 1], None, ALU.mult), a)
            bk.free(a)
            st["ww"] = a

        plan = {}

        def at(U, *fs):
            plan.setdefault(U, []).extend(fs)

        def ln1_at(b, k, U):
            at(U, ln1_load(b, k))
            at(U + 2, ln1_stats(b, k))
            at(U + 3, ln1_norm(b, k))
            at(U + 5, ln1_turn(b, k))

        for b in range(NB + 1):
            B = UB * b
            if b < NB:
                at(B + 0, qk_group(b, 1, 0, 0))
                at(B + 1, qk_group(b, 1, 0, 1))
                at(B + 8, qk_group(b, 1, 1, 0))
                at(B + 9, qk_group(b, 1, 1, 1))
            if b >= 1:
                q = b - 1
                at(B + 2, at_turn(q, 0), at_turn(q, 1), at_turn(q, 2), at_turn(q, 3))
                for k, u in enumerate((3, 5, 6, 7)):
                    at(B + u, proj(q, k))
                at(B + 10, ln2_stats(q))
                for k in range(4):
                    at(B + 11 + k + k // 2, ln2_norm(q, k))
                for k, u in enumerate((14, 14, 18, 18)):
                    at(B + u, x_turn(q, k))
                for t, u in enumerate((17, 18, 19, 20, 21, 22, 23, 25)):
                    at(B + u, enc(q, t))
                for p, (u, v) in enumerate(((27, 30), (31, 35), (36, 39), (40, 45))):
                    at(B + u, gram_c(q, p))
                    at(B + v, gram_a(q, p))
                at(B + 47, select(q))
                at(B + 48, fetch(q))
                for h in range(2):
                    at(B + 53 + 4 * h, mid_mm(q, h))
                    at(B + 54 + 4 * h, out_mm(q, 2 * h))
                    at(B + 55 + 4 * h, out_mm(q, 2 * h + 1))
            if b < NB:
                at(B + 60, prep(b))
            if b == 0:
                at(2, setup_a)
                at(4, setup_b)
                at(6, setup_c)
            if b + 1 < NB:
                for k in range(4):
                    ln1_at(b + 1, k, B + 10 + 5 * k)
                at(B + 33, qk_group(b + 1, 0, 0, 0))
                at(B + 34, qk_group(b + 1, 0, 0, 1))
                at(B + 42, qk_group(b + 1, 0, 1, 0))
                at(B + 43, qk_group(b + 1, 0, 1, 1))
                for k, u in enumerate((49, 50, 51, 56)):
                    at(B + u, v_group(b + 1, k))

        for k in range(4):
            for f in (ln1_load, ln1_stats, ln1_norm, ln1_turn):
                for _ in f(0, k)() or ():
                    pass
        for w in range(2):
            for half in range(2):
                for _ in qk_group(0, 0, w, half)():
                    pass
            move(99)
        for k in range(4):
            for _ in v_group(0, k)():
                pass
        st["w"] = load_ffn_weights()
        n_m = 32 * 8 * NB
        m_next = 0

        def m_some(n):
            nonlocal m_next
            for _ in range(n):
                if m_next < n_m:
                    m_tile(m_next)
                    m_next += 1

        last["M"] = [bk.ev for bk in spare[0:2]]
        use["banks"] = banks + spare[2:]
        m_some(32)
        m_turn(0)
        m_some(4 * LA)

        NU = UB * NB
        last["E"] = [bk.ev for bk in spare[2:]]
        use["banks"] = banks
        going = []

        def step(n=1):
            for _ in range(n):
                while going:
                    try:
                        next(going[0])
                        break
                    except StopIteration:
                        going.pop(0)

        def pieces(fs):
            for f in fs:
                g = f()
                if g is not None:
                    yield from g
                    yield

        for U in range(NU):
            going.append(pieces(plan.get(U, ())))
            if (U + LA) % 8 == MD - 1 and U + LA >= 8:
                turn_at = (U + LA) // 8
            else:
                turn_at = None
            for j in range(4):
                e_tile(U, j)
                m_some(1)
                move(MV)
                if j == MJ and turn_at is not None and turn_at < 2 * 4 * NB:
                    m_turn(turn_at)
                if j == 1 and U % 8 == 1 and U > 1:
                    o_turn(U - 2)
                else:
                    step()
            if U:
                pv(U - 1)
        pv(NU - 1)
        for bk, ev in zip(spare, last["M"] + last["E"]):
            bk.ev = ev
        use["banks"] = banks + spare
        o_turn(NU - 1)
        for U in sorted(k for k in plan if k >= NU):
            going.append(pieces(plan[U]))
        while going:
            step()
        sp.do(lambda e: None, st["x2_out"], ev_modd, inc=False)

        block = ctx.enter_context(nc.Block())

        @block.sync
        def _(e):
            sp.emit(e)

        @block.tensor
        def _(e):
            pe.emit(e)

        @block.vector
        def _(e):
            dve.emit(e)

        @block.scalar
        def _(e):
            act.emit(e)

        @block.gpsimd
        def _(e):
            pool.emit(e)


def kernel(**inputs):
    import numpy as np
    import concourse.bacc as bacc
    from concourse.bass_utils import run_bass_kernel_spmd as run

    g = {k: np.asarray(v) for k, v in inputs.items()}
    p = "L0_ffn_"
    consts = np.zeros((128, 138), np.float32)
    consts[:, 0:128] = np.eye(128)
    consts[:64, 128] = 1
    consts[64:, 129] = 1
    consts[:, 130:138] = np.arange(8)
    wenc = g[p + "W_enc"].transpose(1, 0, 2).reshape(D, NE * H)
    wdec = g[p + "W_dec"].reshape(NE * H, D)
    benc = g[p + "b_enc"].reshape(1, NE * H)
    arrays = [
        ("x", g["L0_attn_x"]), ("wqkvT", g["L0_attn_qkv_w"].T), ("wpT", g["L0_attn_proj_w"].T),
        ("pb", g["L0_attn_proj_b"].reshape(1, D)), ("wbase", g[p + "W_base"]),
        ("bbase", g[p + "b_base"].reshape(1, D)), ("wenc", wenc), ("benc", benc),
        ("bencc", benc.reshape(4, 128).T), ("wdec", wdec), ("wdecT", wdec.T), ("bdecT", g[p + "b_dec"].T),
        ("wdown", g[p + "W_down"]), ("bdown", g[p + "b_down"]), ("wup", g[p + "W_up"]),
        ("bup", g[p + "b_up"]), ("cidx", g[p + "connected_idx"].reshape(1, NE)),
        ("cT", g["L0_c"].T), ("wmod", g["L0_wmod"]), ("consts", consts),
    ]
    arrays = {f"in_{n}": np.ascontiguousarray(a) for n, a in arrays}
    nc = bacc.Bacc("TRN2", target_bir_lowering=False, num_devices=1)
    args = [nc.dram_tensor(n, a.shape, mybir.dt.from_np(a.dtype), kind="ExternalInput").ap()
            for n, a in arrays.items()]
    out = nc.dram_tensor("out_0", (NB, T, D), F, kind="ExternalOutput").ap()
    adaln_block(nc, *args, out)
    r = run(nc, [arrays], core_ids=[0])
    return r.results[0]["out_0"]
```

```python
from contextlib import ExitStack

import concourse.bass as bass
from concourse import mybir

F = mybir.dt.float32
R = mybir.dt.float32r
I32 = mybir.dt.int32
U32 = mybir.dt.uint32
ACT = mybir.ActivationFunctionType
ALU = mybir.AluOpType
AX = mybir.AxisListType

NB, T, D = 4, 1024, 256
NH, HD = 16, 16
NE, H = 8, 64
QC = 48
QM = QC + 2
NEB = 3
LA = 5
LB = 10
SLACK, SLIP = 1.0, 0.3
UB = 64
EPS = 1e-5


class Queue:

    def __init__(self, sem):
        self.sem, self.n, self.ops, self.work = sem, 0, [], 0.0

    def do(self, fn, *after, inc=True, cost=0.25):
        self.work += cost
        self.n += inc
        self.ops.append((after, fn, self.sem if inc else None))
        return (self.sem, self.n)

    def emit(self, eng):
        seen = {}
        for after, fn, sem in self.ops:
            for s, n in after:
                if seen.get(id(s), 0) < n:
                    eng.wait_ge(s, n)
                    seen[id(s)] = n
            ins = fn(eng)
            if sem is not None:
                ins.then_inc(sem, 1)


class Landing:

    def __init__(self, sem):
        self.sem, self.n = sem, 0

    def ev(self):
        return (self.sem, self.n)


def adaln_block(nc, x, wqkvT, wpT, pb, wbase, bbase, wenc, benc, bencc, wdec, wdecT, bdecT,
                wdown, bdown, wup, bup, cidx, cT, wmod, consts, out):
    ctx = ExitStack()
    with ctx:
        def sb(name, shape, dt=F):
            return ctx.enter_context(nc.sbuf_tensor(name, shape, dt))

        def sem(name):
            return ctx.enter_context(nc.semaphore(name))

        pM = ctx.enter_context(nc.psum_tensor("pM", [128, 2, 512], F))
        pE = ctx.enter_context(nc.psum_tensor("pE", [128, NEB, 512], F))
        pO = ctx.enter_context(nc.psum_tensor("pO", [128, 512], F))
        pX = ctx.enter_context(nc.psum_tensor("pX", [128, 5 - NEB, 512], F))
        modd = nc.dram_tensor("modd", [NB, 6 * D], F, kind="Internal").ap()

        QO = sb("QO", [128, 2, 4, T], R)
        KO = sb("KO", [128, 2, 4, T], R)
        V = sb("V", [128, 2, 8, NH, HD + 1])
        P = sb("P", [128, 2, 4, 512])
        hi = sb("hi", [128, T], R)
        lo = sb("lo", [128, T], R)
        osb = sb("osb", [128, 512])
        Atok = sb("Atok", [128, 8, D])
        xin = sb("xin", [128, 2, D])
        h1T = sb("h1T", [128, 2, T])
        h2T = sb("h2T", [128, 2, T])
        x2 = sb("x2", [128, 8, D])
        X = sb("X", [128, 8, D + 2])
        Hb = sb("Hb", [128, 8, 512])
        mid = sb("mid", [128, 512])
        wqkv_s = sb("wqkv_s", [128, 2, 3 * D])
        wp_s = sb("wp_s", [128, 2, D])
        wpg = sb("wpg", [128, 2, D])
        wb_s = sb("wb_s", [128, 2, D])
        wbg = sb("wbg", [128, 2, D])
        wenc_s = sb("wenc_s", [128, 2, 512])
        wd = sb("wd", [128, 4, D + 2])
        ww = sb("ww", [128, 4, 128])
        wdn = sb("wdn", [128, 2, H])
        bdn = sb("bdn", [H, 1])
        wug = sb("wug", [H + 1, D])
        bbr = sb("bbr", [H + 1, D])
        bc = sb("bc", [128, 4, D])
        pbb = sb("pbb", [128, D])
        nbe = sb("nbe", [128, 512])
        cst = sb("cst", [128, 138])
        cT_s = sb("cT_s", [128, 2, NB])
        sg = sb("sg", [128, 3, 2 * NB])
        modT = sb("modT", [128, 4, NB])
        ones = sb("ones", [128, 8])
        st1 = sb("st1", [128, 4, 2, 6])
        mv1 = sb("mv1", [128, 4, 2, 2])
        rs1 = sb("rs1", [128, 4, 2, 2])
        st2 = sb("st2", [128, 8, 6])
        mv2 = sb("mv2", [128, 8, 2])
        rs2 = sb("rs2", [128, 2, 8])
        nh = sb("nh", [128, 8])
        mx = sb("mx", [128, 2, 16, 2])
        mxc = sb("mxc", [128, 16])
        mhl = sb("mhl", [128, 2, 32])
        mh = sb("mh", [128, 16], R)
        mT = sb("mT", [32, 2, 128])
        rec = sb("rec", [128, 4, 4])
        junk = sb("junk", [128, 258])
        junk2 = sb("junk2", [128, 256])
        accC = sb("accC", [128, 4])
        accA = sb("accA", [128, 4])
        ps = sb("ps", [128, 4])
        pl8 = sb("pl8", [128, 4, 2])
        xsq = sb("xsq", [128, 8])
        xsq1 = sb("xsq1", [128, 1])
        xbar = sb("xbar", [128, 2, 2])
        bT = sb("bT", [128, 2, 8])
        bTm = sb("bTm", [128, 2, 8])
        bTq = sb("bTq", [128, 2, 8])
        be = sb("be", [128, 4, 8])
        bec = sb("bec", [128, 4])
        bdT = sb("bdT", [128, 2, 8])
        trow = sb("trow", [1, 8])
        connf = sb("connf", [1, 8])
        conni = sb("conni", [1, 8], I32)
        sel = sb("sel", [1, 8, 8])
        selu = sb("selu", [1, 8], U32)
        seli = sb("seli", [1, 1], I32)

        ident = cst[:, 0:128]
        bmask = cst[:, 128:130]
        iota8 = cst[0:1, 130:138]
        wmod_s = Hb[:, 0:6, :].rearrange("p a b -> p (a b)").rearrange("p (c n) -> p c n", c=2)
        wdT_s = Hb[:, 6:8, :]
        AT = Hb[:, 0:4, :].rearrange("p a b -> p (a b)").rearrange("p (c n) -> p c n", c=2)
        gt = Atok[0:NB, 0:4, :].rearrange("p (a b) n -> p a b n", a=2)
        modr = X[0:NB, :, :].rearrange("p a b -> p (a b)")

        pe, act, dve, pool = (Queue(sem(n)) for n in ("s_pe", "s_act", "s_dve", "s_pool"))
        sp = Queue(None)
        places = {}

        def dma(place, dst, src, *after, q=None):
            if place not in places:
                places[place] = Landing(sem("d_" + place))
            p = places[place]
            p.n += 16
            (q or sp).do(lambda e: e.dma_start(dst, src).then_inc(p.sem, 16), *after, inc=False)
            return p.ev()

        class Bank:

            def __init__(self, t):
                self.t, self.ev, self.held, self.at = t, None, False, 0

            def free(self, ev):
                self.ev, self.held = ev, False

        banks = [Bank(pX[:, i, :]) for i in range(5 - NEB)]
        spare = [Bank(pM[:, i, :]) for i in range(2)] + [Bank(pE[:, i, :]) for i in range(NEB)]
        turn = [0]

        use = {"banks": banks + spare}

        def grab():
            bk = min((x for x in use["banks"] if not x.held), key=lambda x: x.at)
            turn[0] += 1
            bk.held, bk.at = True, turn[0]
            return bk

        def mm(outp, lhsT, rhs, *after, start=True, stop=True, inc=True, skip=False):
            cost = rhs.shape[-1] / 2400 * (1 if rhs.dtype == R else 4 if outp.shape[0] > 32 else 1)
            return pe.do(lambda e: e.matmul(outp, lhsT, rhs, start=start, stop=stop,
                                            skip_group_check=skip), *after, inc=inc, cost=cost)

        def tr(outp, in_, idn, *after, inc=True):
            return pe.do(lambda e: e.transpose(outp, in_, idn), *after, inc=inc, cost=0.11)

        x_tiles = x.rearrange("b (t p) d -> b p t d", p=128)
        def after(*evs):
            return [e for e in evs if e is not None]

        st, last = {}, {}

        h1_ready = [[None] * 4 for _ in range(NB)]
        h1_read = [None]
        xin_free = [None]

        def tokens(b, k):
            return xin[:, :, :] if b else x2[:, 2 * k:2 * k + 2, :]

        def ln1_load(b, k):
            def f():
                last["xin", k] = dma(f"xin{b and 4 or k}", tokens(b, k), x_tiles[b, :, 2 * k:2 * k + 2, :],
                                     *after(xin_free[0] if b else None))
            return f

        def ln1_stats(b, k):
            def f():
                x = tokens(b, k)
                for t in range(2):
                    a = dve.do(lambda e, t=t: e.bn_stats(st1[:, k, t, :], x[:, t, :]), last["xin", k])
                    if t == 0:
                        yield
                for t in range(2):
                    a = dve.do(lambda e, t=t: e.bn_aggr(mv1[:, k, t, :], st1[:, k, t, :]), a)
                a = pool.do(lambda e: e.tensor_scalar(rs1[:, k, 0, :], mv1[:, k, :, 1], EPS, None, ALU.add), a,
                            ev_nh)
                last["rs1", k] = pool.do(lambda e: e.tensor_tensor(rs1[:, k, 1, :], rs1[:, k, 0, :], nh[:, 0:2],
                                                                   ALU.pow), a)
            return f

        def ln1_norm(b, k):
            def f():
                x = tokens(b, k)
                q = pool if b else dve
                for t in range(2):
                    last["xn", k] = q.do(lambda e, t=t: e.tensor_scalar(
                        x[:, t, :], x[:, t, :], mv1[:, k, t, 0:1], rs1[:, k, 1, t:t + 1], ALU.subtract,
                        ALU.mult), last["rs1", k])
            return f

        def ln1_turn(b, k):
            def f():
                x = tokens(b, k)
                bk = grab()
                for c in range(2):
                    for t in range(2):
                        a = tr(bk.t[:, 256 * c + 128 * t:256 * c + 128 * t + 128],
                               x[:, t, 128 * c:128 * c + 128], ident, last["xn", k], ev_cst, *after(bk.ev),
                               inc=c == 1 and t == 1)
                if b:
                    xin_free[0] = a
                else:
                    st["x2_read"] = a
                for c in range(2):
                    g = act.do(lambda e, c=c: e.activation(
                        h1T[:, c, 256 * k:256 * k + 256], bk.t[:, 256 * c:256 * c + 256], ACT.Identity,
                        bias=modT[:, c, b:b + 1], scale=modT[:, 2 + c, b:b + 1]),
                        *after(a, ev_modT, h1_read[0]))
                bk.free(g)
                h1_ready[b][k] = g
            return f

        ev_cst = dma("cst", cst[:, :], consts)
        ev_cT = dma("cT", cT_s[:, :, :], cT.rearrange("(c p) b -> p c b", p=128))
        wmod_c = wmod.rearrange("(c p) n -> p c n", p=128)
        ev_wmod = [dma("wmod0", wmod_s[:, :, 0:512], wmod_c[:, :, 0:512])]
        for k in range(4):
            ln1_load(0, k)()
        ev_wqkv = dma("wqkv", wqkv_s[:, :, :], wqkvT.rearrange("(c p) n -> p c n", p=128))

        def load_ffn_weights():
            evs = [
                dma("w0", wd[:, :, 0:D], wdec.rearrange("(c p) n -> p c n", p=128)),
                dma("w1", wdT_s, wdecT.rearrange("(c p) n -> p c n", p=128)),
                dma("w2", bec[:, :], bencc),
                dma("w3", bdT[:, :, :], bdecT.rearrange("(c p) n -> p c n", p=128)),
                dma("w4", wp_s[:, :, :], wpT.rearrange("(c p) n -> p c n", p=128)),
                dma("w5", wb_s[:, :, :], wbase.rearrange("(c p) n -> p c n", p=128)),
                dma("w6", wenc_s[:, :, :], wenc.rearrange("(c p) n -> p c n", p=128)),
                dma("w7", pbb[:, :], pb.to_broadcast([128, D])),
                dma("w8", nbe[:, :], benc.to_broadcast([128, 512])),
                dma("w9", bbr[H:H + 1, :], bbase),
                dma("w10", conni[:, :], cidx),
            ]
            return evs

        ev_ones = pool.do(lambda e: e.memset(ones[:, :], 1.0))
        ev_nh = pool.do(lambda e: e.memset(nh[:, :], -0.5))
        ev_vone = pool.do(lambda e: e.memset(V[:, :, :, :, HD:], 1.0))
        ev_mid1 = dve.do(lambda e: e.memset(mid[H:H + 1, :], 1.0))
        pf = P[0:2, :, :, :].rearrange("p a b n -> p (a b n)")
        ev_pone = pool.do(lambda e: e.memset(pf, 1.0), ev_vone)
        for half in (0, 1):
            for slot in (0, 1):
                ev_kone = dma("kone", KO[64 * half + QC:64 * half + QM, slot, :, :].bitcast(F), pf, ev_pone)

        ev_po = dve.do(lambda e: e.memset(pO[:, :], 0.0))

        c8 = cT_s[:, :, :].rearrange("p a b -> p (a b)")
        e1 = act.do(lambda e: e.activation(sg[:, 0, :], c8, ACT.Exp, scale=-1.0), ev_cT)
        e2 = dve.do(lambda e: e.tensor_scalar(sg[:, 1, :], sg[:, 0, :], 1.0, None, ALU.add), e1)
        e3 = dve.do(lambda e: e.reciprocal(sg[:, 2, :], sg[:, 1, :]), e2)
        e4 = dve.do(lambda e: e.tensor_tensor(sg[:, 0, :], sg[:, 2, :], c8, ALU.mult), e3)
        mod_ev = {}

        def mod_mm(j):
            bk = grab()
            for c in range(2):
                ev = mm(bk.t[0:NB, :], sg[:, 0, NB * c:NB * c + NB],
                        wmod_s[:, c, 512 * j:512 * j + 512], e4, ev_wmod[min(j, 1)], *after(bk.ev),
                        start=c == 0, stop=c == 1, inc=c == 1)
            mod_ev[j] = act.do(lambda e: e.activation(modr[:, 512 * j:512 * j + 512], bk.t[0:NB, :],
                                                      ACT.Copy), ev)
            bk.free(mod_ev[j])

        mod_mm(0)
        evc = dve.do(lambda e: e.tensor_scalar(modr[:, 256:512], modr[:, 256:512], 1.0, None, ALU.add), mod_ev[0])
        bk0 = grab()
        for k in range(4):
            evt = tr(bk0.t[:, NB * k:NB * k + NB], modr[:, 128 * k:128 * k + 128], ident[0:NB, 0:NB],
                     evc, ev_cst, inc=k == 3)
        ev_modT = dve.do(lambda e: e.tensor_copy(modT[:, :, :].rearrange("p a b -> p (a b)"), bk0.t[:, 0:16]), evt)
        bk0.free(ev_modT)

        def mod_rest():
            mod_mm(1)
            yield
            mod_mm(2)
            yield
            evb = dve.do(lambda e: e.tensor_scalar(modr[:, 1024:1280], modr[:, 1024:1280], 1.0, None, ALU.add),
                         mod_ev[2])
            evg = []
            for k, o in ((0, 512), (1, 1280)):
                a = dve.do(lambda e, k=k, o=o: e.tensor_scalar(gt[:, k, 0, :], modr[:, o:o + 256], 0.0, 2.0,
                                                               ALU.is_ge, ALU.mult), mod_ev[1], mod_ev[2])
                a = dve.do(lambda e, k=k, o=o: e.scalar_tensor_tensor(
                    out=gt[:, k, 1, :], in0=modr[:, o:o + 256], scalar=-1.0, in1=modr[:, o:o + 256],
                    op0=ALU.mult, op1=ALU.max))
                a = dve.do(lambda e, k=k: e.tensor_scalar(gt[:, k, 1, :], gt[:, k, 1, :], 0.25, None, ALU.max), a)
                evg.append(dve.do(lambda e, k=k, o=o: e.scalar_tensor_tensor(
                    out=modr[:, o:o + 256], in0=gt[:, k, 0, :], scalar=-1.0, in1=gt[:, k, 1, :],
                    op0=ALU.add, op1=ALU.mult), a))
            st["gt"] = evg[-1]
            st["modd"] = dma("modd", modd, modr[:, 0:6 * D], evc, evb, *evg)

        last.update({"P": [ev_kone] * 2, "M": None, "pO": ev_po,
                "hilo_in": [None, None]})

        oct_ready = {}
        moving = []

        def move(n):
            for _ in range(n):
                while moving:
                    try:
                        next(moving[0])
                        break
                    except StopIteration:
                        moving.pop(0)

        e_done = {}

        def qk_group(b, o, w, half):
            def f():
                bk = grab()
                r0 = 256 * w + 128 * o
                for c in range(2):
                    a = mm(bk.t[:, :], wqkv_s[:, c, r0:r0 + 128], h1T[:, c, 512 * half:512 * half + 512],
                           ev_wqkv, *after(bk.ev), h1_ready[b][2 * half + 1], start=c == 0, stop=c == 1,
                           inc=c == 1)
                    if c == 0:
                        yield
                h1_read[0] = a
                cs = slice(512 * half, 512 * half + 512)
                sc = 0.25 if w == 0 else 1.0
                hi_, lo_ = hi, lo
                if (b, o, w) == (0, 0, 1):
                    hi_, lo_ = h2T[:, 0, :].bitcast(R), h2T[:, 1, :].bitcast(R)
                else:
                    assert half or not moving
                a = act.do(lambda e: e.activation(hi_[:, cs], bk.t[:, :], ACT.Copy, scale=sc),
                           *after(a, *last["hilo_in"]))
                a = dve.do(lambda e: e.scalar_tensor_tensor(out=lo_[:, cs], in0=bk.t[:, :], scalar=sc,
                                                            in1=hi_[:, cs].bitcast(F), op0=ALU.mult,
                                                            op1=ALU.subtract), a)
                bk.free(a)
                if half == 1:
                    slot = (2 * b + o) % 2
                    dst = KO if w else QO
                    parts = (hi_, lo_, hi_) if w else (hi_, hi_, lo_)
                    n = 2 * b + o
                    evs = after(a, ev_kone, e_done.get(n - 2))

                    def copies(g):
                        for h in range(4 * g, 4 * g + 4):
                            for r in range(3):
                                p0 = 64 * (h % 2) + 16 * r
                                first = n == 0 and w
                                ev = dma(f"op{w}{slot}{g}" + "p" * first, dst[p0:p0 + 16, slot, h // 2, :].bitcast(F),
                                         parts[r][16 * h:16 * h + 16, :].bitcast(F), *evs,
                                         q=pool if first else sp)
                                yield
                        oct_ready[(2 * n + g, w)] = ev
                        if hi_ is hi:
                            last["hilo_in"][g] = ev
                    moving.extend((copies(0), copies(1)))
            return f

        v_ready = {}
        pv_done = {}

        def v_group(b, k):
            def f():
                bk = grab()
                for t in range(2):
                    for c in range(2):
                        tt = 2 * k + t
                        a = mm(bk.t[:, 256 * t:256 * t + 256], h1T[:, c, 128 * tt:128 * tt + 128],
                               wqkv_s[:, c, 512:768], ev_wqkv, *after(bk.ev), h1_ready[b][k],
                               start=c == 0, stop=c == 1, inc=c == 1 and t == 1)
                    if t == 0:
                        yield
                h1_read[0] = a
                a = act.do(lambda e: e.activation(V[:, b % 2, 2 * k:2 * k + 2, :, 0:HD],
                                                  bk.t[:, :].rearrange("p (t h e) -> p t h e", t=2, e=HD), ACT.Copy),
                           *after(a, pv_done.get(b - 2)))
                bk.free(a)
                v_ready[(b, k)] = a
            return f

        m_last = {}
        m_rows = {}
        mx_free = [None, None]

        def operand(buf, gi, j, rows, sl):
            base = 64 * (j % 2)
            return buf[base:base + rows, (gi // 2) % 2, 2 * (gi % 2) + j // 2, sl]

        def m_tile(i):
            hq, k = divmod(i, 32)
            gi, c = divmod(hq, 2)
            k, kh = divmod(k, 2)
            j, qb = divmod(k, 4)
            s = i % len(last["M"])
            t = (pM[:, s, :] if s < 2 else pE[:, s - 2, :])
            q0 = 512 * c + 128 * qb
            a = mm(t, operand(QO, gi, j, QC, slice(q0, q0 + 128)),
                   operand(KO, gi, j, QC, slice(512 * kh, 512 * kh + 512)), *after(last["M"][s]),
                   oct_ready[(gi, 0)], oct_ready[(gi, 1)])
            g = dve.do(lambda e: e.tensor_reduce(mx[:, hq % 2, k:k + 1, kh], t, AX.X, ALU.max,
                                                 negate=True), *after(a, mx_free[hq % 2]), cost=0.62)
            last["M"][s] = g
            if i % 32 == 31:
                v = mx[:, hq % 2, :, :]
                a = dve.do(lambda e: e.tensor_tensor(mxc[:, :], v[:, :, 0], v[:, :, 1], ALU.min), g)
                a = pool.do(lambda e: e.tensor_copy(mh[:, :], mxc[:, :]), a)
                pool.do(lambda e: e.tensor_copy(mhl[:, hq % 2, 0:16], mh[:, :].bitcast(F)), a)
                m_last[hq] = pool.do(lambda e: e.tensor_tensor(mhl[:, hq % 2, 16:32], mxc[:, :],
                                                              mh[:, :].bitcast(F), ALU.subtract), a)
                mx_free[hq % 2] = m_last[hq]

        def m_turn(hq):
            bk = grab()
            gi, c = divmod(hq, 2)
            a = tr(bk.t[0:32, 0:128], mhl[:, hq % 2, :], ident, m_last[hq], *after(bk.ev))
            mx_free[hq % 2] = a
            a = act.do(lambda e: e.activation(mT[:, hq % 2, :], bk.t[0:32, 0:128], ACT.Copy),
                       *after(a, *(m_rows.get((hq - 2, j)) for j in range(4))))
            bk.free(a)
            for j in range(4):
                for r in range(2):
                    p0 = 64 * (j % 2) + QC + r
                    dst = QO[p0:p0 + 1, (gi // 2) % 2, 2 * (gi % 2) + j // 2, 512 * c:512 * c + 512]
                    m_rows[(hq, j)] = dma(f"m{hq % 2}{j}", dst.rearrange("p (a b) -> p a b", a=4).bitcast(F),
                             mT[16 * r + 4 * j:16 * r + 4 * j + 4, hq % 2, :], a)

        e_count = [0]
        exp_ev = {}

        def e_tile(U, j):
            gi, u = divmod(U, 16)
            c, kb = divmod(u, 8)
            s = e_count[0] % NEB
            e_count[0] += 1
            a = mm(pE[:, s, :], operand(KO, gi, j, QM, slice(128 * kb, 128 * kb + 128)),
                   operand(QO, gi, j, QM, slice(512 * c, 512 * c + 512)),
                   *after(m_rows[(2 * gi + c, j)], last["E"][s], oct_ready[(gi, 0)], oct_ready[(gi, 1)]))
            e_done[gi // 2] = a
            g = act.do(lambda e: e.activation(P[:, U % 2, j, :], pE[:, s, :], ACT.Exp),
                       *after(a, last["P"][U % 2]))
            last["E"][s] = g
            exp_ev[U] = g

        def pv(U):
            gi, u = divmod(U, 16)
            kb = u % 8
            b = gi // 4
            for j in range(4):
                h = 4 * (gi % 4) + j
                a = mm(pO[32 * j:32 * j + HD + 1, :], V[:, b % 2, kb, h, :], P[:, U % 2, j, :],
                       *after(exp_ev[U], v_ready[(b, kb // 2)], ev_vone, last["pO"] if kb == 0 else None),
                       start=kb == 0, stop=kb == 7, inc=j == 3)
            last["P"][U % 2] = a
            pv_done[b] = a
            if kb == 7:
                a = act.do(lambda e: e.activation(osb[:, :], pO[:, :], ACT.Copy), *after(a, last.get("osb")))
                last["pO"] = a
                last["osb_in"] = a

        at_ev = {}

        def o_turn(U):
            bk = grab()
            gi, u = divmod(U, 16)
            c, b, g = u // 8, gi // 4, gi % 4
            for k in range(4):
                a = tr(bk.t[:, 128 * k:128 * k + 128], osb[:, 128 * k:128 * k + 128], ident,
                       last["osb_in"], *after(bk.ev), inc=k == 3)
            last["osb"] = a
            v = bk.t[:, :].rearrange("p (k j e) -> p k j e", k=4, j=4)
            a = dve.do(lambda e: e.reciprocal(rec[:, :, :], v[:, :, :, HD]), a)
            dst = Atok[:, 4 * c:4 * c + 4, 64 * g:64 * g + 64].rearrange("p k (j e) -> p k j e", j=4)
            a = dve.do(lambda e: e.tensor_tensor(
                dst, v[:, :, :, 0:HD], rec[:, :, :].unsqueeze(3).to_broadcast([128, 4, 4, HD]), ALU.mult),
                *after(a, at_ev.get((b - 1, 3)), st["gt"]))
            bk.free(a)
            last["Atok"] = a


        def at_turn(b, k):
            def f():
                bk = grab()
                c, th = k // 2, k % 2
                for t in range(4):
                    a = tr(bk.t[:, 128 * t:128 * t + 128], Atok[:, 4 * th + t, 128 * c:128 * c + 128], ident,
                           last["Atok"], *after(bk.ev), inc=t == 3)
                at_ev[(b, k)] = a
                a = act.do(lambda e: e.activation(AT[:, c, 512 * th:512 * th + 512], bk.t[:, :], ACT.Copy),
                           *after(a, st.get("Hread"), st.get("setup")))
                bk.free(a)
                st["AT"] = a
            return f

        def prep(b):
            def f():
                for k, o in enumerate((512, 768, 1024, 1280)):
                    st["bc"] = dma("bc", bc[:, k, :], modd[b:b + 1, o:o + 256].to_broadcast([128, 256]),
                                   *after(st["modd"], st.get("bc_read")))
                ev = dma("x2", x2[:, :, :], x_tiles[b], *after(st.get("x2_out"), st["x2_read"]))
                ga = bc[:, 0:1, :].to_broadcast([128, 2, D])
                gb = bc[:, 3:4, :].to_broadcast([128, 2, D])
                a = pool.do(lambda e: e.tensor_tensor(wpg[:, :, :], wp_s[:, :, :], ga, ALU.mult),
                            *after(st["bc"], st["w"][4], st.get("proj")))
                a = pool.do(lambda e: e.tensor_tensor(bc[:, 0, :], pbb[:, :], bc[:, 0, :], ALU.mult), a,
                            st["w"][7])
                pool.do(lambda e: e.tensor_tensor(wbg[:, :, :], wb_s[:, :, :], gb, ALU.mult), st["w"][5],
                        *after(st.get("outmm")))
                for t in range(8):
                    st["x2"] = pool.do(lambda e, t=t: e.tensor_tensor(x2[:, t, :], x2[:, t, :], bc[:, 0, :],
                                                                      ALU.add), ev, a)
            return f

        def proj(b, k):
            def f():
                bk = grab()
                for t in range(2):
                    for c in range(2):
                        tt = 2 * k + t
                        a = mm(bk.t[:, 256 * t:256 * t + 256], AT[:, c, 128 * tt:128 * tt + 128], wpg[:, c, :],
                               st["AT"], st["x2"], *after(bk.ev), start=c == 0, stop=c == 1,
                               inc=c == 1 and t == 1)
                    if t == 0:
                        yield
                st["proj"] = a
                sl = x2[:, 2 * k:2 * k + 2, :]
                a = dve.do(lambda e: e.tensor_tensor(sl, bk.t[:, :].rearrange("p (t n) -> p t n", t=2), sl,
                                                     ALU.add), a)
                bk.free(a)
                for t in range(2):
                    yield
                    st[("st2", k)] = dve.do(lambda e, t=t: e.bn_stats(st2[:, 2 * k + t, :], x2[:, 2 * k + t, :]), a)
            return f

        def ln2_stats(b, k):
            def f():
                if (b, k) == (0, 0):
                    st["xone"] = pool.do(lambda e: e.memset(X[:, :, D:D + 2], 1.0), st["modd"], evt)
                t0 = 2 * k
                for t in (t0, t0 + 1):
                    a = dve.do(lambda e, t=t: e.bn_aggr(mv2[:, t, :], st2[:, t, :]), st[("st2", k)])
                a = pool.do(lambda e: e.tensor_scalar(rs2[:, 0, t0:t0 + 2], mv2[:, t0:t0 + 2, 1], EPS, None,
                                                      ALU.add), a)
                st[("rs2", k)] = pool.do(lambda e: e.tensor_tensor(rs2[:, 1, t0:t0 + 2], rs2[:, 0, t0:t0 + 2],
                                                                   nh[:, 0:2], ALU.pow), a)
            return f

        def ln2_norm(b, k):
            def f():
                evs = []
                for t in (2 * k, 2 * k + 1):
                    if t % 2:
                        yield
                    evs.append(dve.do(lambda e, t=t: e.scalar_tensor_tensor(
                        out=X[:, t, 0:D], in0=x2[:, t, :], scalar=mv2[:, t, 0:1], in1=bc[:, 2, :],
                        op0=ALU.subtract, op1=ALU.mult), *after(st[("rs2", k)], st["bc"], st.get("Xread"), st["modd"], evt)))
                for i, t in enumerate((2 * k, 2 * k + 1)):
                    yield
                    a = dve.do(lambda e, t=t: e.scalar_tensor_tensor(
                        out=X[:, t, 0:D], in0=X[:, t, 0:D], scalar=rs2[:, 1, t:t + 1], in1=bc[:, 1, :],
                        op0=ALU.mult, op1=ALU.add), evs[i])
                    st[("X", t)] = a
                for t in (2 * k, 2 * k + 1):
                    yield
                    g = act.do(lambda e, t=t: e.activation(junk2[:, :], X[:, t, 0:D], ACT.Square,
                                                           accum_out=xsq[:, t:t + 1]),
                               *after(st[("X", t)], st.get("xsq"), st.get("xsq_read")))
                    st["xsq"] = g
            return f

        def x_turn(b, k):
            def f():
                bk = grab()
                c, th = k % 2, k // 2
                for t in range(4):
                    a = tr(bk.t[:, 128 * t:128 * t + 128], X[:, 4 * th + t, 128 * c:128 * c + 128], ident,
                           st[("X", 4 * th + t)], *after(bk.ev), inc=t == 3)
                a = act.do(lambda e: e.activation(h2T[:, c, 512 * th:512 * th + 512], bk.t[:, :], ACT.Identity,
                                                  accum_out=xbar[:, c, th:th + 1]),
                           *after(a, st.get("outmm"), st.get("Lmm"), oct_ready[(0, 1)], oct_ready[(1, 1)]))
                bk.free(a)
                st[("h2T", th)] = a
            return f

        def enc(b, t):
            def f():
                bk = grab()
                for c in range(2):
                    a = mm(bk.t[:, :], h2T[:, c, 128 * t:128 * t + 128], wenc_s[:, c, :], st[("h2T", t // 4)],
                           st["w"][6], *after(bk.ev), start=c == 0, stop=c == 1, inc=c == 1)
                    if c == 0:
                        yield
                a = dve.do(lambda e: e.tensor_tensor(Hb[:, t, :], bk.t[:, :], nbe[:, :], ALU.max),
                           *after(a, st["nbe"], st["proj"], st.get("Hread")))
                bk.free(a)
                st["H"] = a
            return f

        def gram_c(b, p):
            def f():
                bk = grab()
                for t in range(8):
                    a = mm(bk.t[:, 0:D + 2], Hb[:, t, 128 * p:128 * p + 128], X[:, t, :], st["H"], *after(bk.ev),
                           st["xone"], start=t == 0, stop=t == 7, inc=t == 7)
                    if t in (1, 3, 5):
                        yield
                st["Xread"] = a
                a = dve.do(lambda e: e.tensor_tensor_reduce(junk[:, :], bk.t[:, 0:D + 2], wd[:, p, :], 1.0, 0.0,
                                                            ALU.mult, ALU.add, accC[:, p:p + 1]),
                           *after(a, st["wd"], st.get("junk"), st.get("acc_read")))
                bk.free(a)
                st["junk"] = a
            return f

        def gram_a(b, p):
            def f():
                bk = grab()
                for t in range(8):
                    a = mm(bk.t[:, 0:128], Hb[:, t, 128 * p:128 * p + 128], Hb[:, t, 128 * p:128 * p + 128],
                           st["H"], *after(bk.ev), start=t == 0, stop=t == 7, inc=t == 7)
                    if t == 3:
                        yield
                st["Hread"] = a
                a = dve.do(lambda e: e.tensor_tensor_reduce(junk[:, 0:128], bk.t[:, 0:128], ww[:, p, :], 1.0, 0.0,
                                                            ALU.mult, ALU.add, accA[:, p:p + 1]),
                           *after(a, st["ww"], st.get("junk"), st.get("acc_read")))
                bk.free(a)
                st["junk"] = a
            return f

        def select(b):
            def f():
                a = dve.do(lambda e: e.tensor_tensor(ps[:, :], accC[:, :], accA[:, :], ALU.add),
                           *after(st["junk"], st.get("Lmm")))
                st["acc_read"] = a
                g = dve.do(lambda e: e.tensor_reduce(xsq1[:, :], xsq[:, :], AX.X, ALU.add),
                           *after(st["xsq"], st.get("Lmm")))
                st["xsq_read"] = g
                a = dve.do(lambda e: e.tensor_tensor(
                    pl8[:, :, :], ps[:, :].unsqueeze(2).to_broadcast([128, 4, 2]),
                    bmask.unsqueeze(1).to_broadcast([128, 4, 2]), ALU.mult), a)
                yield
                yield
                yield
                bk = grab()
                L = bk.t[0:1, 0:8]
                mm(L, ones[:, 0:1], pl8[:, :, :].rearrange("p a b -> p (a b)"), a, *after(bk.ev), ev_ones,
                   stop=False, inc=False)
                for c in range(2):
                    for th in range(2):
                        mm(L, xbar[:, c, th:th + 1], bTm[:, c, :], st[("h2T", 0)], st[("h2T", 1)], st["bTm"],
                           start=False, stop=False, inc=False)
                mm(L, xsq1[:, 0:1], ones[:, :], g, start=False, stop=False, inc=False)
                a = mm(L, ones[0:1, 0:1], trow[:, :], st["trow"], start=False)
                st["Lmm"] = a
                a = dve.do(lambda e: e.tensor_scalar(sel[:, 0, :], L, -1.0 / (T * D), None, ALU.mult),
                           *after(a, st.get("seli_read")))
                bk.free(a)
                a = dve.do(lambda e: e.max(sel[:, 1, :], sel[:, 0, :]), a)
                a = dve.do(lambda e: e.max_index(selu[:, :], sel[:, 1, :], sel[:, 0, :]), a)
                a = dve.do(lambda e: e.tensor_copy(sel[:, 2, 0:1], selu[:, 0:1]), a)
                a = dve.do(lambda e: e.tensor_scalar(sel[:, 3, :], iota8, sel[:, 2, 0:1], None, ALU.is_equal), a)
                a = dve.do(lambda e: e.tensor_tensor_reduce(sel[:, 4, :], sel[:, 3, :], connf[:, :], 1.0, 0.0,
                                                            ALU.mult, ALU.add, sel[:, 5, 0:1]),
                           a, st["conn"])
                a = dve.do(lambda e: e.tensor_scalar(sel[:, 5, 1:2], sel[:, 5, 0:1], 0.0, 8.0, ALU.is_lt,
                                                     ALU.mult), a)
                a = dve.do(lambda e: e.tensor_tensor(sel[:, 5, 2:3], sel[:, 5, 0:1], sel[:, 5, 1:2], ALU.add), a)
                a = dve.do(lambda e: e.tensor_scalar(seli[:, :], sel[:, 5, 2:3], 0.0, 7.0, ALU.max, ALU.min), a)
                st["idx"] = a
            return f

        def fetch(b):
            def f():
                vals = {}

                def dyn(place, dst, src, *evs):
                    if place not in places:
                        places[place] = Landing(sem("d_" + place))
                    p = places[place]
                    p.n += 16
                    sp.do(lambda e: e.dma_start(dst, src(vals["v"])).then_inc(p.sem, 16), *evs, inc=False)
                    return p.ev()

                def load(e):
                    vals["v"] = e.value_load(seli[0:1, 0:1], min_val=0, max_val=7)
                sp.do(load, st["idx"], inc=False)
                w = after(st.get("midmm"), st.get("outmm"), st.get("relu"))
                e1 = dyn("sel", wdn[:, :, :], lambda v: wdown[bass.ds(v, 1), :, :].rearrange(
                    "a (c p) r -> p (a c) r", p=128), *w)
                e1 = dyn("sel", bdn[:, :], lambda v: bdown[bass.ds(v, 1), :].rearrange("a r -> r a"))
                e1 = dyn("sel", wug[0:H, :], lambda v: wup[bass.ds(v, 1), :, :].rearrange("a r n -> (a r) n"))
                e1 = dyn("sel", wug[H:H + 1, :], lambda v: bup[bass.ds(v, 1), :])
                st["sel"] = e1
                a = pool.do(lambda e: e.tensor_tensor(wug[H:H + 1, :], wug[H:H + 1, :], bbr[H:H + 1, :],
                                                     ALU.add), e1, st["w"][9])
                a = pool.do(lambda e: e.tensor_tensor(wug[:, :], wug[:, :], bc[0:H + 1, 3, :], ALU.mult), a)
                st["wug"] = a
                st["seli_read"] = e1
                st["bc_read"] = a
            return f

        def mid_mm(b, half):
            def f():
                bk = grab()
                for c in range(2):
                    a = mm(bk.t[0:H, :], wdn[:, c, :], h2T[:, c, 512 * half:512 * half + 512], st["sel"],
                           *after(bk.ev), start=c == 0, stop=c == 1, inc=c == 1)
                    if c == 0:
                        yield
                st["midmm"] = a
                a = act.do(lambda e: e.activation(mid[0:H, :], bk.t[0:H, :], ACT.Relu, bias=bdn[:, 0:1]),
                           *after(a, st.get("outmm")))
                bk.free(a)
                st["mid"] = a
                st["relu"] = a
            return f

        def out_base(k, t, bk):
            tt = 2 * k + t
            for c in range(2):
                mm(bk.t[:, 256 * t:256 * t + 256], h2T[:, c, 128 * tt:128 * tt + 128], wbg[:, c, :],
                   *after(bk.ev), st["x2"], start=c == 0, stop=False, inc=False)
            return bk

        def base_first():
            for k in range(4):
                st[("base", k)] = out_base(k, 0, grab())

        def out_mm(b, k):
            def f():
                bk = st.pop(("base", k), None) or out_base(k, 0, grab())
                for t in range(2):
                    tt = 2 * k + t
                    o = bk.t[:, 256 * t:256 * t + 256]
                    if t:
                        out_base(k, 1, bk)
                    m0 = 128 * (tt % 4)
                    a = mm(o, mid[0:H + 1, m0:m0 + 128], wug[:, :], st["mid"], st["wug"], ev_mid1,
                           start=False, inc=t == 1)
                    if t == 0:
                        yield
                st["outmm"] = a
                sl = x2[:, 2 * k:2 * k + 2, :]
                a = dve.do(lambda e: e.tensor_tensor(sl, bk.t[:, :].rearrange("p (t n) -> p t n", t=2), sl,
                                                     ALU.add), a)
                bk.free(a)
                st["x2_out"] = dma("out", out.rearrange("b (t p) d -> b p t d", p=128)[b, :, 2 * k:2 * k + 2, :],
                                   sl, a)
            return f

        def setup_a():
            bk = grab()
            a = dve.do(lambda e: e.memset(be[:, :, :], 0.0))
            for p in range(4):
                g = dve.do(lambda e, p=p: e.tensor_scalar(be[:, p, 2 * p:2 * p + 2], bmask, bec[:, p:p + 1],
                                                          None, ALU.mult), a, st["w"][2], ev_cst)
            for c in range(2):
                for p in range(4):
                    a = mm(bk.t[:, 8 * c:8 * c + 8], wd[:, p, 128 * c:128 * c + 128], be[:, p, :], g,
                           st["w"][0], *after(bk.ev), start=p == 0, stop=p == 3, inc=p == 3)
            a = dve.do(lambda e: e.tensor_tensor(bT[:, :, :], bk.t[:, 0:16].rearrange("p (c n) -> p c n", c=2),
                                                 bdT[:, :, :], ALU.add), a, st["w"][3])
            bk.free(a)
            st["bT"] = a
            st["bTm"] = dve.do(lambda e: e.tensor_scalar(bTm[:, :, :], bT[:, :, :], -2.0, None, ALU.mult), a)
            st["bTq"] = dve.do(lambda e: e.tensor_tensor(bTq[:, :, :], bT[:, :, :], bT[:, :, :], ALU.mult))
            a = dve.do(lambda e: e.tensor_copy(connf[:, :], conni[:, :]), st["w"][10])
            st["conn"] = a
            st["nbe"] = dve.do(lambda e: e.tensor_scalar(nbe[:, :], nbe[:, :], -1.0, None, ALU.mult), st["w"][8])

        def setup_b():
            bk = grab()
            for p in range(4):
                for c in range(2):
                    a = mm(bk.t[:, 8 * p:8 * p + 8], wdT_s[:, c, 128 * p:128 * p + 128], bT[:, c, :], st["bT"],
                           st["w"][1], *after(bk.ev), start=c == 0, stop=c == 1, inc=c == 1)
            for p in range(4):
                g = dve.do(lambda e, p=p: e.scalar_tensor_tensor(
                    out=pl8[:, p, :], in0=bk.t[:, 10 * p:10 * p + 2], scalar=2.0, in1=bmask, op0=ALU.mult,
                    op1=ALU.mult), a)
            bk.free(g)
            g = dve.do(lambda e: e.tensor_reduce(wd[:, :, D], pl8[:, :, :], AX.X, ALU.add), g)
            g = dve.do(lambda e: e.memset(wd[:, :, D + 1], 0.0))
            st["wd"] = dve.do(lambda e: e.tensor_scalar(wd[:, :, 0:D], wd[:, :, 0:D], -2.0, None, ALU.mult),
                              st["bT"])
            bk2 = grab()
            for c in range(2):
                a = mm(bk2.t[0:1, 0:8], ones[:, 0:1], bTq[:, c, :], st["bTq"], *after(bk2.ev), start=c == 0,
                       stop=c == 1, inc=c == 1)
            a = dve.do(lambda e: e.tensor_scalar(trow[:, :], bk2.t[0:1, 0:8], float(T), None, ALU.mult), a)
            bk2.free(a)
            st["trow"] = a

        def setup_c():
            bk = grab()
            for p in range(4):
                for c in range(2):
                    w = wdT_s[:, c, 128 * p:128 * p + 128]
                    a = mm(bk.t[:, 128 * p:128 * p + 128], w, w, *after(bk.ev), st["w"][1], start=c == 0,
                           stop=c == 1, inc=c == 1)
            st["setup"] = a
            for k in range(2):
                a = dve.do(lambda e, k=k: e.tensor_scalar(
                    ww[:, :, 64 * k:64 * k + 64], bk.t[:, :].rearrange("p (a b) -> p a b", a=4)[:, :, 64 * k:64 * k + 64],
                    bmask[:, k:k + 1], None, ALU.mult), a)
            bk.free(a)
            st["ww"] = a

        plan = {}

        def at(U, *fs):
            plan.setdefault(U, []).extend(fs)

        def ln1_at(b, k, U):
            at(U, ln1_load(b, k))
            at(U + 2, ln1_stats(b, k))
            at(U + 3, ln1_norm(b, k))
            at(U + 5, ln1_turn(b, k))

        for b in range(NB + 1):
            B = UB * b
            if b < NB:
                if b == 0:
                    at(0, v_group(0, 2))
                    at(1, v_group(0, 3))
                if b:
                    at(B + 0, qk_group(b, 1, 0, 0))
                    at(B + 1, qk_group(b, 1, 0, 1))
                at(B + 8, qk_group(b, 1, 1, 0))
                at(B + 9, qk_group(b, 1, 1, 1))
            if b >= 1:
                q = b - 1
                at(B + 2, at_turn(q, 2), at_turn(q, 3))
                for k, u in enumerate((3, 5, 6, 7)):
                    at(B + u, proj(q, k))
                    if q == NB - 1 and k > 0:
                        at(B + u, ln2_stats(q, k - 1))
                    if q == NB - 1 and k > 1:
                        at(B + u, ln2_norm(q, k - 2))
                for k in range(4):
                    if q < NB - 1 or k == 3:
                        at(B + 9, ln2_stats(q, k))
                    if q < NB - 1 or k > 1:
                        at(B + 12 + k + k // 2, ln2_norm(q, k))
                for k, u in enumerate((15, 15, 19, 19)):
                    at(B + u, x_turn(q, k))
                for t, u in enumerate((17, 18, 19, 20, 22, 23, 24, 25)):
                    at(B + u, enc(q, t))
                for p, (u, v) in enumerate(((27, 30), (31, 35), (36, 39), (40, 45))):
                    at(B + u, gram_c(q, p))
                    at(B + v, gram_a(q, p))
                at(B + 47, select(q))
                at(B + 48, fetch(q))
                if q == NB - 1:
                    at(B + 49, base_first)
                for h in range(2):
                    at(B + 53 + 4 * h, mid_mm(q, h))
                    at(B + 54 + 4 * h, out_mm(q, 2 * h))
                    at(B + 55 + 4 * h, out_mm(q, 2 * h + 1))
            if b < NB:
                at(B + 55, at_turn(b, 0))
                at(B + 56, at_turn(b, 1))
                at(B + 60, prep(b))
            if b + 1 < NB:
                for k in range(4):
                    ln1_at(b + 1, k, B + 9 + 5 * k)
                at(B + 33, qk_group(b + 1, 0, 0, 0))
                at(B + 34, qk_group(b + 1, 0, 0, 1))
                at(B + 42, qk_group(b + 1, 0, 1, 0))
                at(B + 43, qk_group(b + 1, 0, 1, 1))
                for k, u in enumerate((49, 50, 51, 56) if b else (18, 23, 29, 40)):
                    at(B + u, v_group(b + 1, k))

        ev_wmod.append(dma("wmod1", wmod_s[:, :, 512:], wmod_c[:, :, 512:]))
        st["w"] = load_ffn_weights()
        for k in range(4):
            for _ in ln1_stats(0, k)():
                pass
        for k in range(4):
            ln1_norm(0, k)()
            ln1_turn(0, k)()
        for w in range(2):
            for half in range(2):
                for _ in qk_group(0, 0, w, half)():
                    pass
        moving[1], moving[2] = moving[2], moving[1]
        move(49)
        n_m = 32 * 8 * NB
        m_next = 0

        def m_some(n):
            nonlocal m_next
            for _ in range(n):
                if m_next < n_m:
                    m_tile(m_next)
                    m_next += 1

        going = []

        def step(n=1):
            for _ in range(n):
                while going:
                    try:
                        next(going[0])
                        break
                    except StopIteration:
                        going.pop(0)

        def pieces(fs):
            for f in fs:
                g = f()
                if g is not None:
                    yield from g
                    yield

        use["banks"] = banks
        going.append(pieces([v_group(0, 0), v_group(0, 1), mod_rest, setup_a, setup_b, setup_c]))
        step(99)
        last["M"] = [bk.ev for bk in spare]
        m_some(32)
        last["M"], last["E"] = last["M"][0:2], last["M"][2:]
        m_turn(0)
        going.append(pieces([qk_group(0, 1, 0, 0), qk_group(0, 1, 0, 1)]))
        step(99)

        NU = UB * NB
        use["banks"] = banks
        turned = 1
        for U in range(NU):
            m_ready = m_next // 32
            going.append(pieces(plan.get(U, ())))
            for j in range(4):
                e_tile(U, j)
                n = 4 * U + j + 1
                lead = m_next - 32 - n
                dve.work = max(dve.work, pe.work - SLACK)
                pe.work = max(pe.work, dve.work - SLACK)
                m_some(min(n // 2, 4 * LA) - lead)
                if m_next - 32 - n < 4 * LB and dve.work < pe.work + SLIP:
                    m_some(1)
                move(1)
                if j == 2 and turned < m_ready:
                    m_turn(turned)
                    turned += 1
                if j == 1 and U % 8 == 1 and U > 1:
                    o_turn(U - 2)
                else:
                    step()
            if U:
                pv(U - 1)
        pv(NU - 1)
        for bk, ev in zip(spare, last["M"] + last["E"]):
            bk.ev = ev
        use["banks"] = banks + spare
        o_turn(NU - 1)
        for U in sorted(k for k in plan if k >= NU):
            going.append(pieces(plan[U]))
        while going:
            step()
        sp.do(lambda e: None, st["x2_out"], st["modd"], inc=False)

        block = ctx.enter_context(nc.Block())

        @block.sync
        def _(e):
            sp.emit(e)

        @block.tensor
        def _(e):
            pe.emit(e)

        @block.vector
        def _(e):
            dve.emit(e)

        @block.scalar
        def _(e):
            act.emit(e)

        @block.gpsimd
        def _(e):
            pool.emit(e)


def kernel(**inputs):
    import numpy as np
    import concourse.bacc as bacc
    from concourse.bass_utils import run_bass_kernel_spmd as run

    g = {k: np.asarray(v) for k, v in inputs.items()}
    p = "L0_ffn_"
    consts = np.zeros((128, 138), np.float32)
    consts[:, 0:128] = np.eye(128)
    consts[:64, 128] = 1
    consts[64:, 129] = 1
    consts[:, 130:138] = np.arange(8)
    wenc = g[p + "W_enc"].transpose(1, 0, 2).reshape(D, NE * H)
    wdec = g[p + "W_dec"].reshape(NE * H, D)
    benc = g[p + "b_enc"].reshape(1, NE * H)
    arrays = [
        ("x", g["L0_attn_x"]), ("wqkvT", g["L0_attn_qkv_w"].T), ("wpT", g["L0_attn_proj_w"].T),
        ("pb", g["L0_attn_proj_b"].reshape(1, D)), ("wbase", g[p + "W_base"]),
        ("bbase", g[p + "b_base"].reshape(1, D)), ("wenc", wenc), ("benc", benc),
        ("bencc", benc.reshape(4, 128).T), ("wdec", wdec), ("wdecT", wdec.T), ("bdecT", g[p + "b_dec"].T),
        ("wdown", g[p + "W_down"]), ("bdown", g[p + "b_down"]), ("wup", g[p + "W_up"]),
        ("bup", g[p + "b_up"]), ("cidx", g[p + "connected_idx"].reshape(1, NE)),
        ("cT", g["L0_c"].T), ("wmod", g["L0_wmod"]), ("consts", consts),
    ]
    arrays = {f"in_{n}": np.ascontiguousarray(a) for n, a in arrays}
    nc = bacc.Bacc("TRN2", target_bir_lowering=False, num_devices=1)
    args = [nc.dram_tensor(n, a.shape, mybir.dt.from_np(a.dtype), kind="ExternalInput").ap()
            for n, a in arrays.items()]
    out = nc.dram_tensor("out_0", (NB, T, D), F, kind="ExternalOutput").ap()
    adaln_block(nc, *args, out)
    r = run(nc, [arrays], core_ids=[0])
    return r.results[0]["out_0"]
```
